# Optimizing a Trainium2 kernel written in Bass

```python
import numpy as np
import jax
import jax.numpy as jnp

def _softmax(x, axis=-1):
    return jax.nn.softmax(x, axis=axis)

def _gelu(x):
    return jax.nn.gelu(x, approximate=True)

def _silu(x):
    return jax.nn.silu(x)

def _sigmoid(x):
    return jax.nn.sigmoid(x)

def _layernorm(x, axis=-1, eps=1e-05):
    m = jnp.mean(x, axis=axis, keepdims=True)
    v = jnp.var(x, axis=axis, keepdims=True)
    return (x - m) / jnp.sqrt(v + eps)

def _scatter_add(tgt, idx, src, axis=0):
    return tgt.at[idx].add(src)

def _segment_sum(src, seg, n):
    return jax.ops.segment_sum(src, seg, n)
kernel_name = 'mk_macaron_d1_jaxref_r4_623bad'

def setup_inputs(seed: int=0):
    np.random.seed(seed)
    _w = jnp.asarray

    def _L0_attn_setup():
        import jax, jax.numpy as jnp
        import numpy as np
        from jax import lax
        HIDDEN = 512
        INTER = 1024
        NHEADS = 64
        HEADDIM = INTER // NHEADS
        STATE = 128
        NGROUPS = 1
        CONVK = 4
        CHUNK = 64
        CONV_DIM = INTER + 2 * NGROUPS * STATE
        EPS = 1e-05
        DT_MIN, DT_MAX = (0.0, 100.0)

        def _segsum(x):
            l = x.shape[-1]
            xx = jnp.broadcast_to(x[..., None], x.shape + (l,))
            m1 = jnp.tril(jnp.ones((l, l), bool), -1)
            s = jnp.cumsum(jnp.where(m1, xx, 0.0), axis=-2)
            m2 = jnp.tril(jnp.ones((l, l), bool), 0)
            return jnp.where(m2, s, -jnp.inf)
        key = jax.random.key(seed)
        ks = jax.random.split(key, 4)
        B, S = (1, 1024)
        std = 0.02
        return {'hidden_states': jax.random.normal(ks[0], (B, S, HIDDEN), jnp.float32), 'in_proj_w': jax.random.normal(ks[1], (INTER + CONV_DIM + NHEADS, HIDDEN), jnp.float32) * std, 'conv_w': jax.random.normal(ks[2], (CONV_DIM, 1, CONVK), jnp.float32) * std, 'conv_b': jnp.zeros((CONV_DIM,), jnp.float32), 'dt_bias': jnp.ones((NHEADS,), jnp.float32), 'A_log': jnp.log(jnp.arange(1, NHEADS + 1, dtype=jnp.float32)), 'D': jnp.ones((NHEADS,), jnp.float32), 'norm_w': jnp.ones((INTER,), jnp.float32), 'out_proj_w': jax.random.normal(ks[3], (HIDDEN, INTER), jnp.float32) * std}
    _L0_attn_in = _L0_attn_setup()

    def _L0_ffn_setup():
        import jax, jax.numpy as jnp
        import numpy as np
        HIDDEN = 512
        INTER = 2048
        SCALE = 64.0

        def fwht(x):
            orig_shape = x.shape
            n = orig_shape[-1]
            x = x.reshape(-1, n)
            h = 1
            while h < n:
                x = x.reshape(-1, n // (2 * h), 2, h)
                a, b = (x[:, :, 0, :], x[:, :, 1, :])
                x = jnp.stack([a + b, a - b], axis=2).reshape(-1, n)
                h *= 2
            return (x / jnp.sqrt(jnp.asarray(n, x.dtype))).reshape(orig_shape)
        key = jax.random.key(seed)
        ks = jax.random.split(key, 8)
        inp = jax.random.normal(ks[0], (4, 512, HIDDEN), dtype=jnp.float32)
        SU_ug = jnp.where(jax.random.bernoulli(ks[1], 0.5, (HIDDEN,)), 1.0, -1.0).astype(jnp.float32)
        SU_dp = jnp.where(jax.random.bernoulli(ks[2], 0.5, (INTER,)), 1.0, -1.0).astype(jnp.float32)
        Wscale_ug = jax.random.uniform(ks[3], (2 * INTER,), jnp.float32, 0.5, 1.5)
        Wscale_dp = jax.random.uniform(ks[4], (HIDDEN,), jnp.float32, 0.5, 1.5)
        W_up = jax.random.normal(ks[5], (INTER, HIDDEN), dtype=jnp.float32) * 0.02
        W_gate = jax.random.normal(ks[6], (INTER, HIDDEN), dtype=jnp.float32) * 0.02
        W_down = jax.random.normal(ks[7], (HIDDEN, INTER), dtype=jnp.float32) * 0.02
        return {'input': inp, 'SU_ug': SU_ug, 'SU_dp': SU_dp, 'Wscale_ug': Wscale_ug, 'Wscale_dp': Wscale_dp, 'W_up': W_up, 'W_gate': W_gate, 'W_down': W_down}
    _L0_ffn_in = _L0_ffn_setup()
    _d = {'L0_attn_hidden_states': _L0_attn_in['hidden_states'], 'L0_attn_in_proj_w': _L0_attn_in['in_proj_w'], 'L0_attn_conv_w': _L0_attn_in['conv_w'], 'L0_attn_conv_b': _L0_attn_in['conv_b'], 'L0_attn_dt_bias': _L0_attn_in['dt_bias'], 'L0_attn_A_log': _L0_attn_in['A_log'], 'L0_attn_D': _L0_attn_in['D'], 'L0_attn_norm_w': _L0_attn_in['norm_w'], 'L0_attn_out_proj_w': _L0_attn_in['out_proj_w'], 'L0_ffn_SU_ug': _L0_ffn_in['SU_ug'], 'L0_ffn_SU_dp': _L0_ffn_in['SU_dp'], 'L0_ffn_Wscale_ug': _L0_ffn_in['Wscale_ug'], 'L0_ffn_Wscale_dp': _L0_ffn_in['Wscale_dp'], 'L0_ffn_W_up': _L0_ffn_in['W_up'], 'L0_ffn_W_gate': _L0_ffn_in['W_gate'], 'L0_ffn_W_down': _L0_ffn_in['W_down']}
    _x0 = _d['L0_attn_hidden_states']
    _d['L0_attn_hidden_states'] = jax.random.normal(jax.random.fold_in(jax.random.key(seed), 1), (4, 512, 512), dtype=_x0.dtype)
    del _x0
    return _d

def reference(L0_attn_hidden_states, L0_attn_in_proj_w, L0_attn_conv_w, L0_attn_conv_b, L0_attn_dt_bias, L0_attn_A_log, L0_attn_D, L0_attn_norm_w, L0_attn_out_proj_w, L0_ffn_SU_ug, L0_ffn_SU_dp, L0_ffn_Wscale_ug, L0_ffn_Wscale_dp, L0_ffn_W_up, L0_ffn_W_gate, L0_ffn_W_down):

    def _L0_attn_ref(hidden_states, in_proj_w, conv_w, conv_b, dt_bias, A_log, D, norm_w, out_proj_w):
        import jax, jax.numpy as jnp
        import numpy as np
        from jax import lax
        HIDDEN = 512
        INTER = 1024
        NHEADS = 64
        HEADDIM = INTER // NHEADS
        STATE = 128
        NGROUPS = 1
        CONVK = 4
        CHUNK = 64
        CONV_DIM = INTER + 2 * NGROUPS * STATE
        EPS = 1e-05
        DT_MIN, DT_MAX = (0.0, 100.0)

        def _segsum(x):
            l = x.shape[-1]
            xx = jnp.broadcast_to(x[..., None], x.shape + (l,))
            m1 = jnp.tril(jnp.ones((l, l), bool), -1)
            s = jnp.cumsum(jnp.where(m1, xx, 0.0), axis=-2)
            m2 = jnp.tril(jnp.ones((l, l), bool), 0)
            return jnp.where(m2, s, -jnp.inf)
        Bsz, S, _ = hidden_states.shape
        proj = hidden_states @ in_proj_w.T
        gate, xBC, dt = jnp.split(proj, [INTER, INTER + CONV_DIM], axis=-1)
        xBC_t = xBC.transpose(0, 2, 1)
        xBC_t = lax.conv_general_dilated(xBC_t, conv_w, (1,), [(CONVK - 1, 0)], dimension_numbers=('NCH', 'OIH', 'NCH'), feature_group_count=CONV_DIM)
        xBC = jax.nn.silu((xBC_t + conv_b[None, :, None]).transpose(0, 2, 1))
        x, Bmat, Cmat = jnp.split(xBC, [INTER, INTER + NGROUPS * STATE], axis=-1)
        A = -jnp.exp(A_log.astype(jnp.float32))
        dt = jnp.clip(jax.nn.softplus(dt + dt_bias), DT_MIN, DT_MAX)
        x = x.reshape(Bsz, S, NHEADS, HEADDIM).astype(jnp.float32)
        Bmat = jnp.tile(Bmat.reshape(Bsz, S, NGROUPS, STATE).astype(jnp.float32), (1, 1, NHEADS // NGROUPS, 1))
        Cmat = jnp.tile(Cmat.reshape(Bsz, S, NGROUPS, STATE).astype(jnp.float32), (1, 1, NHEADS // NGROUPS, 1))
        pad = (CHUNK - S % CHUNK) % CHUNK
        D_res = D[..., None] * jnp.pad(x, ((0, 0), (0, pad), (0, 0), (0, 0)))
        x = x * dt[..., None]
        Adt = A * dt

        def chunk(t):
            t = jnp.pad(t, ((0, 0), (0, pad)) + ((0, 0),) * (t.ndim - 2))
            return t.reshape(t.shape[0], -1, CHUNK, *t.shape[2:])
        x_c, A_c, B_c, C_c = (chunk(x), chunk(Adt), chunk(Bmat), chunk(Cmat))
        A_c = A_c.transpose(0, 3, 1, 2)
        A_cum = jnp.cumsum(A_c, axis=-1)
        L = jnp.exp(_segsum(A_c))
        G = jnp.einsum('bclhn,bcshn->bclsh', C_c, B_c)
        M = G * L.transpose(0, 2, 3, 4, 1)
        Y_diag = jnp.einsum('bclsh,bcshp->bclhp', M, x_c)
        decay_states = jnp.exp(A_cum[..., -1:] - A_cum)
        B_decay = B_c * decay_states.transpose(0, 2, 3, 1)[..., None]
        states = jnp.einsum('bclhn,bclhp->bchpn', B_decay, x_c)
        states = jnp.concatenate([jnp.zeros_like(states[:, :1]), states], axis=1)
        decay_chunk = jnp.exp(_segsum(jnp.pad(A_cum[..., -1], ((0, 0), (0, 0), (1, 0)))))
        new_states = jnp.einsum('bhzj,bjhpn->bzhpn', decay_chunk, states)
        states = new_states[:, :-1]
        state_decay_out = jnp.exp(A_cum).transpose(0, 2, 3, 1)
        Y_off = jnp.einsum('bclhn,bchpn->bclhp', C_c, states) * state_decay_out[..., None]
        y = (Y_diag + Y_off).reshape(Bsz, -1, NHEADS, HEADDIM) + D_res
        y = y[:, :S].reshape(Bsz, S, INTER)
        y = y * jax.nn.silu(gate)
        var = jnp.mean(jnp.square(y), axis=-1, keepdims=True)
        y = y * lax.rsqrt(var + EPS) * norm_w
        return y @ out_proj_w.T

    def _L0_ffn_ref(input, SU_ug, SU_dp, Wscale_ug, Wscale_dp, W_up, W_gate, W_down):
        import jax, jax.numpy as jnp
        import numpy as np
        HIDDEN = 512
        INTER = 2048
        SCALE = 64.0

        def fwht(x):
            orig_shape = x.shape
            n = orig_shape[-1]
            x = x.reshape(-1, n)
            h = 1
            while h < n:
                x = x.reshape(-1, n // (2 * h), 2, h)
                a, b = (x[:, :, 0, :], x[:, :, 1, :])
                x = jnp.stack([a + b, a - b], axis=2).reshape(-1, n)
                h *= 2
            return (x / jnp.sqrt(jnp.asarray(n, x.dtype))).reshape(orig_shape)
        n = SU_ug.shape[0]
        x = input.reshape(-1, n)
        x = fwht(x * SU_ug) / SCALE
        x_up = x @ W_up.T * (Wscale_ug[:INTER] * SCALE)
        x_gate = x @ W_gate.T * (Wscale_ug[INTER:] * SCALE)
        x = jax.nn.silu(x_gate) * x_up
        x = fwht(x * SU_dp) / SCALE
        x = x @ W_down.T * (Wscale_dp * SCALE)
        return x.reshape(input.shape)
    x = L0_attn_hidden_states
    x = x + 0.5 * _L0_ffn_ref(_layernorm(x, axis=-1), L0_ffn_SU_ug, L0_ffn_SU_dp, L0_ffn_Wscale_ug, L0_ffn_Wscale_dp, L0_ffn_W_up, L0_ffn_W_gate, L0_ffn_W_down)
    x = x + _L0_attn_ref(_layernorm(x, axis=-1), L0_attn_in_proj_w, L0_attn_conv_w, L0_attn_conv_b, L0_attn_dt_bias, L0_attn_A_log, L0_attn_D, L0_attn_norm_w, L0_attn_out_proj_w)
    x = x + 0.5 * _L0_ffn_ref(_layernorm(x, axis=-1), L0_ffn_SU_ug, L0_ffn_SU_dp, L0_ffn_Wscale_ug, L0_ffn_Wscale_dp, L0_ffn_W_up, L0_ffn_W_gate, L0_ffn_W_down)
    return x

_drawn_inputs = setup_inputs


def setup_inputs(seed=0):
    import zlib

    import numpy as np

    out = dict(_drawn_inputs(seed))
    spreads = {'L0_attn_conv_b': (0.0, 0.1),
     'L0_attn_dt_bias': (1.0, 0.2),
     'L0_attn_D': (1.0, 0.2),
     'L0_attn_norm_w': (1.0, 0.2)}
    factors = {}
    for name, (base, spread) in spreads.items():
        noise = np.random.default_rng([zlib.crc32(name.encode()), seed]).standard_normal(out[name].shape)
        drawn = base * np.exp(spread * noise) if base else spread * noise
        out[name] = jnp.asarray(drawn.astype(out[name].dtype))
    for name, factor in factors.items():
        out[name] = (out[name] * factor).astype(out[name].dtype)
    return out
```

```python
from contextlib import ExitStack
import math

import numpy as np
import concourse.bass as bass
from concourse import mybir

F32 = mybir.dt.float32
F32R = mybir.dt.float32r
ALU = mybir.AluOpType
ACT = mybir.ActivationFunctionType

P = 128
BATCH, SEQ, HID = 4, 512, 512
TOK = BATCH * SEQ
NT = TOK // P
KH = HID // P
FF = 2048
CH = 256
NC = FF // CH
FB = FF // P
G = TOK // 512
TPG = 512 // P
INTER, STATE, HEADS, HDIM = 1024, 128, 64, 16
NB = INTER // P
HPB = P // HDIM
NIN = 2 * NB + 3
BI_B, BI_C, BI_DT = 2 * NB, 2 * NB + 1, 2 * NB + 2
NCK = SEQ // P
EPS = 1e-5

C_H, C_I4, C_I2, C_END = 0, P, P + 4 * P, P + 4 * P + HEADS
_c = np.cumsum([0, KH, FB, 1, 1, NB, 40, 10, NB, HID]).tolist()
P_SUG, P_SUD, P_ALOG, P_DTB, P_D, P_CW, P_CB, P_NW, P_WDP, P_END = _c

PASSES = ((0, 0), (0, 1), (1, 0))


def wait(eng, sem, value):
    if isinstance(value, int) and value <= 0:
        return
    eng.wait_ge(sem, value)


class Chain:

    def __init__(self, eng, sem, base=0):
        self.eng, self.sem, self.n, self.base = eng, sem, 0, base

    def done(self, ins):
        self.n += 1
        ins.then_inc(self.sem, 1)

    def sync(self):
        wait(self.eng, self.sem, self.base + self.n)

    def step(self, ins):
        self.done(ins)
        self.sync()


def program(nc, x, wug, wsc, wdn, win, wout, cst, par, out):
    ug_s = nc.dram_tensor("ug_split", [NC, P, 2 * KH * 2 * CH], F32, kind="Internal").ap()
    dn_s = nc.dram_tensor("dn_split", [NC, P, 2 * 2 * HID], F32, kind="Internal").ap()
    in_s = nc.dram_tensor("in_split", [NIN + 1, P, 2 * HID], F32, kind="Internal").ap()
    out_s = nc.dram_tensor("out_split", [NB, P, 2 * HID], F32, kind="Internal").ap()
    with ExitStack() as ctx:
        res = ctx.enter_context(nc.sbuf_tensor("res", [P, NT, HID], F32))
        cs = ctx.enter_context(nc.sbuf_tensor("cs", [P, C_END], F32))
        pr = ctx.enter_context(nc.sbuf_tensor("pr", [P, P_END], F32))
        sug = ctx.enter_context(nc.sbuf_tensor("sug", [P, KH], F32))
        sud = ctx.enter_context(nc.sbuf_tensor("sud", [P, FB], F32))
        acol = ctx.enter_context(nc.sbuf_tensor("acol", [P, 1], F32))
        i2r = ctx.enter_context(nc.sbuf_tensor("i2r", [P, HEADS], F32R))
        ones = ctx.enter_context(nc.sbuf_tensor("ones", [P, P], F32))
        banks = [ctx.enter_context(nc.psum_tensor(f"bank{i}", [P, 512], F32)) for i in range(8)]
        s = dict(res=res, cs=cs, pr=pr, sug=sug, sud=sud, acol=acol, i2r=i2r, ones=ones, banks=banks)
        prepare(nc, s, x, wug, wdn, win, wout, cst, par, ug_s, dn_s, in_s, out_s)
        ffn(nc, s, "a", ug_s, dn_s, wsc)
        mixer(nc, s, in_s, out_s)
        ffn(nc, s, "b", ug_s, dn_s, wsc)
        store(nc, s, out)


def store(nc, s, out):
    with ExitStack() as ctx:
        s_out = ctx.enter_context(nc.semaphore("st_out"))
        block = ctx.enter_context(nc.Block())

        @block.sync
        def _(sp):
            sp.dma_start(out.rearrange("(t p) n -> p t n", p=P), s["res"][:]).then_inc(s_out, 16)
            sp.wait_ge(s_out, 16)


def prepare(nc, s, x, wug, wdn, win, wout, cst, par, ug_s, dn_s, in_s, out_s):
    res, cs, pr, banks = s["res"], s["cs"], s["pr"], s["banks"]
    with ExitStack() as ctx:
        def sb(name, shape, dt=F32):
            return ctx.enter_context(nc.sbuf_tensor(name, shape, dt))

        def sem(name):
            return ctx.enter_context(nc.semaphore(name))

        raw = sb("p_raw", [P, 2, KH, 512])
        t1 = sb("p_t1", [P, 2, KH, 512])
        t2 = sb("p_t2", [P, 2, KH, 512])
        wo = sb("p_wo", [P, 2, 2, KH, 512], F32R)
        da = sb("p_da", [P, FB, HID])
        db = sb("p_db", [P, FB, HID])
        sc = sb("p_sc", [P, 2, HID])
        s_par, s_x, s_d = sem("p_par"), sem("p_x"), sem("p_d")
        s_raw = [sem("p_raw0"), sem("p_raw1")]
        s_t1, s_t2, s_mm, s_hi, s_lo = sem("p_t1s"), sem("p_t2s"), sem("p_mm"), sem("p_hi"), sem("p_lo")
        s_st = [sem("p_st0"), sem("p_st1")]
        s_c, s_bf, s_dm, s_dsc, s_dhi, s_dlo = (sem(f"p_{n}") for n in ("c", "bf", "dm", "dsc", "dhi", "dlo"))
        s_ex, s_chi, s_clo = sem("p_ex"), sem("p_chi"), sem("p_clo")
        H = cs[:, C_H:C_H + P]
        NP = 7
        STAGES = FB.bit_length() - 1
        QD = FB // 4
        block = ctx.enter_context(nc.Block())

        def stored(eng, piece):
            wait(eng, s_st[piece % 2], 16 * (piece // 2 + 1) if piece >= 0 else 0)

        def ext(i):
            return (win if i < 5 else wout), (in_s if i < 5 else out_s), (i if i < 5 else i - 5)

        def put_ext(sp, i):
            piece = NC + i
            _, dst, at = ext(i)
            sp.dma_start(dst[4 * at:4 * at + 4].rearrange("b p (h n) -> p h b n", h=2),
                         wo[:, piece % 2].bitcast(F32)).then_inc(s_st[piece % 2], 16)

        def down_stored(eng, q):
            piece = NC + NP + q
            par_ = piece % 2
            before = (piece - 2) // 2 + 1 if q < 2 else (NC + NP + 1 - par_) // 2 + 2 * (q // 2)
            wait(eng, s_st[par_], 16 * before)

        @block.sync
        def _(sp):
            sp.dma_start(cs[:], cst).then_inc(s_par, 16)
            sp.dma_start(pr[:], par).then_inc(s_par, 16)
            for c in range(NC):
                wait(sp, s_t1, 2 * (c - 1))
                sp.dma_start(raw[:, c % 2], wug[c].rearrange("p (k n) -> p k n", k=KH)).then_inc(s_raw[c % 2], 16)
                if c == 0:
                    sp.dma_start(da[:], wdn.rearrange("p (k n) -> p k n", k=FB)).then_inc(s_d, 16)
                    sp.dma_start(res[:], x.rearrange("(t p) n -> p t n", p=P)).then_inc(s_x, 16)
                if c >= 2:
                    wait(sp, s_lo, KH * (c - 1))
                    sp.dma_start(ug_s[c - 2], wo[:, c % 2].rearrange("p h k n -> p (h k n)").bitcast(F32)).then_inc(s_st[c % 2], 16)
            for i in range(NP):
                piece = NC + i
                src, _, at = ext(i)
                if i < 2:
                    wait(sp, s_t1, 2 * (NC - 1 + i))
                else:
                    wait(sp, s_clo, i - 1)
                sp.dma_start(raw[:, piece % 2], src[4 * at:4 * at + 4].rearrange("b p n -> p b n")).then_inc(s_raw[piece % 2], 16)
                if i < 2:
                    wait(sp, s_lo, KH * (NC - 1 + i))
                    sp.dma_start(ug_s[NC - 2 + i], wo[:, piece % 2].rearrange("p h k n -> p (h k n)").bitcast(F32)).then_inc(s_st[piece % 2], 16)
                else:
                    put_ext(sp, i - 2)
            for i in (NP - 2, NP - 1):
                wait(sp, s_clo, i + 1)
                put_ext(sp, i)
            for q in range(QD):
                piece = NC + NP + q
                wait(sp, s_dlo, 4 * (q + 1))
                for h in range(2):
                    dst = dn_s[2 * q + h].rearrange("p (l j n) -> p l j n", l=2, j=2)
                    sp.dma_start(dst, wo[:, piece % 2, :, 2 * h:2 * h + 2, :].bitcast(F32)).then_inc(s_st[piece % 2], 16)
            sp.wait_ge(s_x, 16)
            total0 = 16 * (8 + 2 * 2)
            total1 = 16 * (7 + 2 * 2)
            sp.wait_ge(s_st[0], total0)
            sp.wait_ge(s_st[1], total1)

        @block.gpsimd
        def _(pool):
            for c in range(NC):
                wait(pool, s_raw[c % 2], 16 * (c // 2 + 1))
                wait(pool, s_t2, 2 * (c - 1))
                for n, op in enumerate((ALU.add, ALU.subtract)):
                    pool.tensor_tensor(t1[:, c % 2, n::2, :], raw[:, c % 2, 0::2, :], raw[:, c % 2, 1::2, :], op).then_inc(s_t1, 1)

        @block.tensor
        def _(pe):
            pe.wait_ge(s_par, 32)
            for c in range(NC):
                pe.wait_ge(s_t2, 2 * (c + 1))
                for k in range(KH):
                    wait(pe, s_lo, KH * (c - 2) + k + 1)
                    pe.matmul(banks[4 * (c % 2) + k][:], H, t2[:, c % 2, k, :], start=True, stop=True).then_inc(s_mm, 1)
            src = da if STAGES % 2 == 0 else db
            pe.wait_ge(s_bf, 2 * STAGES)
            for j in range(FB):
                if j < 8:
                    pe.wait_ge(s_lo, KH * (NC - 2) + j + 1)
                else:
                    pe.wait_ge(s_dsc, j - 7)
                pe.matmul(banks[j % 8][:], H, src[:, j, :], start=True, stop=True).then_inc(s_dm, 1)

        @block.scalar
        def _(act):
            act.wait_ge(s_par, 32)
            act.activation(s["acol"][:], pr[:, P_ALOG:P_ALOG + 1], ACT.Exp).then_inc(s_ex, 1)
            act.wait_ge(s_c, 4)
            for c in range(NC):
                stored(act, c - 2)
                for k in range(KH):
                    act.wait_ge(s_mm, KH * c + k + 1)
                    act.activation(wo[:, c % 2, 0, k, :], banks[4 * (c % 2) + k][:], ACT.Copy,
                                   scale=s["sug"][:, k:k + 1]).then_inc(s_hi, 1)
            for i in range(NP):
                piece = NC + i
                act.wait_ge(s_raw[piece % 2], 16 * (piece // 2 + 1))
                stored(act, piece - 2)
                for k in range(4):
                    scale = pr[:, P_NW + 4 * (i - 5) + k:P_NW + 4 * (i - 5) + k + 1] if i >= 5 else 1.0
                    act.activation(wo[:, piece % 2, 0, k, :], raw[:, piece % 2, k, :], ACT.Copy,
                                   scale=scale).then_inc(s_chi, 1)
            for j in range(FB):
                q = j // 4
                if j % 4 == 0:
                    down_stored(act, q)
                act.wait_ge(s_dsc, j + 1)
                act.copy(wo[:, (NC + NP + q) % 2, 0, j % 4, :], sc[:, j % 2, :]).then_inc(s_dhi, 1)

        @block.vector
        def _(dve):
            dve.memset(s["ones"][:], 1.0).then_inc(s_c, 1)
            dve.wait_ge(s_par, 32)
            dve.tensor_scalar(s["sug"][:], pr[:, P_SUG:P_SUG + KH], 1.0 / math.sqrt(HID), None, ALU.mult).then_inc(s_c, 1)
            dve.tensor_scalar(s["sud"][:], pr[:, P_SUD:P_SUD + FB], 0.5 / math.sqrt(FF), None, ALU.mult).then_inc(s_c, 1)
            dve.tensor_copy(s["i2r"][:], cs[:, C_I2:C_I2 + HEADS]).then_inc(s_c, 1)
            dve.wait_ge(s_ex, 1)
            dve.tensor_scalar(s["acol"][:], s["acol"][:], -1.0, None, ALU.mult).then_inc(s_c, 1)
            dve.wait_ge(s_c, 5)

            def butterfly(st):
                a, b = (da, db) if st % 2 == 0 else (db, da)
                w = 1 << st
                src = a[:].rearrange("p (u t w) n -> p u t (w n)", t=2, w=w)
                dst = b[:].rearrange("p (u t w) n -> p u t (w n)", t=2, w=w)
                wait(dve, s_bf, 2 * st)
                for t, op in enumerate((ALU.add, ALU.subtract)):
                    dve.tensor_tensor(dst[:, :, t, :], src[:, :, 0, :], src[:, :, 1, :], op).then_inc(s_bf, 1)

            dve.wait_ge(s_d, 16)
            for c in range(NC + 1):
                if c < NC:
                    dve.wait_ge(s_t1, 2 * (c + 1))
                    wait(dve, s_mm, KH * (c - 1))
                    for n, op in enumerate((ALU.add, ALU.subtract)):
                        dve.tensor_tensor(t2[:, c % 2, 2 * n:2 * n + 2, :], t1[:, c % 2, 0:2, :], t1[:, c % 2, 2:4, :], op).then_inc(s_t2, 1)
                if c < STAGES:
                    butterfly(c)
                if c >= 1:
                    for k in range(KH):
                        dve.wait_ge(s_hi, KH * (c - 1) + k + 1)
                        dve.scalar_tensor_tensor(wo[:, (c - 1) % 2, 1, k, :], banks[4 * ((c - 1) % 2) + k][:],
                                                 s["sug"][:, k:k + 1], wo[:, (c - 1) % 2, 0, k, :].bitcast(F32),
                                                 ALU.mult, ALU.subtract).then_inc(s_lo, 1)
            for i in range(NP):
                piece = NC + i
                dve.wait_ge(s_chi, 4 * (i + 1))
                for k in range(4):
                    scale = pr[:, P_NW + 4 * (i - 5) + k:P_NW + 4 * (i - 5) + k + 1] if i >= 5 else 1.0
                    ins = dve.scalar_tensor_tensor(wo[:, piece % 2, 1, k, :], raw[:, piece % 2, k, :], scale,
                                                   wo[:, piece % 2, 0, k, :].bitcast(F32), ALU.mult, ALU.subtract)
                ins.then_inc(s_clo, 1)
            for j in range(FB + 1):
                if j < FB:
                    dve.wait_ge(s_dm, j + 1)
                    wait(dve, s_dlo, j - 1)
                    dve.scalar_tensor_tensor(sc[:, j % 2, :], banks[j % 8][:], s["sud"][:, j:j + 1],
                                             pr[:, P_WDP:P_WDP + HID], ALU.mult, ALU.mult).then_inc(s_dsc, 1)
                if j >= 1:
                    i = j - 1
                    dve.wait_ge(s_dhi, i + 1)
                    o = wo[:, (NC + NP + i // 4) % 2, :, i % 4, :]
                    dve.tensor_tensor(o[:, 1, :], sc[:, i % 2, :], o[:, 0, :].bitcast(F32), ALU.subtract).then_inc(s_dlo, 1)


def rsqrt(eng, ch, y, v, t, scale=1.0):
    I32 = mybir.dt.int32
    ch.step(eng.tensor_scalar(v, v, scale, EPS, ALU.mult, ALU.add))
    ch.step(eng.tensor_scalar(y.bitcast(I32), v.bitcast(I32), 1, None, ALU.arith_shift_right))
    ch.done(eng.tensor_scalar(v, v, -0.5, None, ALU.mult))
    ch.sync()
    ch.step(eng.tensor_scalar(y.bitcast(I32), y.bitcast(I32), -1.0, float(0x5F3759DF), ALU.mult, ALU.add))
    for _ in range(4):
        ch.step(eng.tensor_tensor(t, y, y, ALU.mult))
        ch.step(eng.tensor_tensor(t, t, v, ALU.mult))
        ch.step(eng.scalar_tensor_tensor(y, t, 1.5, y, ALU.add, ALU.mult))


def normalize(dve, st, mv, xn, tiles, ch, free):
    for i, t in enumerate(tiles):
        ch.done(dve.bn_stats(st[:, i, :], t))
    ch.sync()
    mean, var, d, rstd = (mv[:, i, :] for i in range(4))
    ch.done(dve.tensor_tensor(mean, st[:, :, 1], st[:, :, 4], ALU.add))
    ch.done(dve.tensor_tensor(var, st[:, :, 2], st[:, :, 5], ALU.add))
    ch.step(dve.tensor_tensor(d, st[:, :, 1], st[:, :, 4], ALU.subtract))
    ch.done(dve.tensor_scalar(mean, mean, 0.5, None, ALU.mult))
    ch.step(dve.scalar_tensor_tensor(d, d, 0.25, d, ALU.mult, ALU.mult))
    ch.step(dve.scalar_tensor_tensor(var, var, 1.0 / HID, d, ALU.mult, ALU.add))
    rsqrt(dve, ch, rstd, var, d)
    for i, t in enumerate(tiles):
        sem = free(i)
        dve.tensor_scalar(xn[:, i, :], t, mean[:, i:i + 1], rstd[:, i:i + 1], ALU.subtract, ALU.mult).then_inc(sem, 1)


def ffn(nc, s, tag, ug_s, dn_s, wsc):
    res, cs, banks = s["res"], s["cs"], s["banks"]
    with ExitStack() as ctx:
        def sb(name, shape, dt=F32):
            return ctx.enter_context(nc.sbuf_tensor(f"f{tag}_{name}", shape, dt))

        def sem(name):
            return ctx.enter_context(nc.semaphore(f"f{tag}_{name}"))

        xT = sb("xT", [P, 2, KH, TOK], F32R)
        xn = sb("xn", [P, TPG, HID])
        st, mv = sb("st", [P, TPG, 6]), sb("mv", [P, 4, TPG])
        wu = [sb(f"wu{i}", [P, 2, KH, 2 * CH], F32R) for i in range(2)]
        wd = [sb(f"wd{i}", [P, 2, 2, HID], F32R) for i in range(2)]
        sc = [sb(f"sc{i}", [P, 4], F32) for i in range(2)]
        sil = sb("sil", [P, 2, 512])
        hf = sb("hf", [P, 2, 512])
        hb = sb("hb", [P, 2, 2, 2, 512], F32R)
        s_wu = [sem("wu0s"), sem("wu1s")]
        s_wd = [sem("wd0s"), sem("wd1s")]
        s_u, s_sil, s_h, s_hi, s_lo, s_d, s_acc = (sem(n) for n in ("u", "sils", "h", "hi", "lo", "d", "acc"))
        s_own, s_xn, s_tr, s_xhi, s_xlo = (sem(n) for n in ("own", "xns", "tr", "xhi", "xlo"))
        U, D, T = banks[0:4], banks[4:6], banks[6:8]
        block = ctx.enter_context(nc.Block())

        @block.sync
        def _(sp):
            def load(c, p):
                wait(sp, s_d, 16 * (c - 1))
                wait(sp, s_wu[p], 0 if isinstance(c, int) else 32)
                for dst, src, landed in ((wu[p][:].rearrange("p h k n -> p (h k n)").bitcast(F32), ug_s, s_wu),
                                         (sc[p][:], wsc, s_wu),
                                         (wd[p][:].rearrange("p h k n -> p (h k n)").bitcast(F32), dn_s, s_wd)):
                    sp.dma_start(dst, src[bass.ds(c, 1)].rearrange("c p n -> (c p) n")).then_inc(landed[p], 16)
            load(0, 0)
            load(1, 1)
            with sp.Fori(1, NC // 2) as c2:
                load(2 * c2, 0)
                load(2 * c2 + 1, 1)

        @block.tensor
        def _(pe):
            def turn(g):
                for i in range(TPG):
                    t = TPG * g + i
                    pe.wait_ge(s_xn, t + 1)
                    wait(pe, s_xlo, t - 1)
                    for k in range(KH):
                        ins = pe.transpose(T[i % 2][:, k * P:(k + 1) * P], xn[:, i, k * P:(k + 1) * P], cs[:, C_I4:C_I4 + P])
                    ins.then_inc(s_tr, 1)

            def up(n, c2, m):
                g, p = m % 4, m // 4
                if isinstance(n, int) and n < 4:
                    pe.wait_ge(s_xlo, TPG * (g + 1))
                if g == 0:
                    pe.wait_ge(s_wu[p], 32 * c2 + 32)
                for j in range(4):
                    wait(pe, s_sil if j < 2 else s_h, 2 * n - 1 + j % 2)
                    for k in range(KH):
                        for a, b in PASSES:
                            ins = pe.matmul(U[j][:], wu[p][:, a, k, j * P:(j + 1) * P], xT[:, b, k, g * 512:(g + 1) * 512],
                                            start=(k == 0 and (a, b) == PASSES[0]), stop=(k == KH - 1 and (a, b) == PASSES[-1]))
                    ins.then_inc(s_u, 1)

            def down(n, c2, m):
                g, p = m % 4, m // 4
                if g == 0:
                    pe.wait_ge(s_wd[p], 16 * c2 + 16)
                pe.wait_ge(s_lo, 2 * n + 2)
                for t in range(TPG):
                    wait(pe, s_acc, 4 * n + t - 1)
                    for j in range(2):
                        for a, b in PASSES:
                            ins = pe.matmul(D[t % 2][:], hb[:, m % 2, a, j, t * P:(t + 1) * P], wd[p][:, b, j, :],
                                            start=(j == 0 and (a, b) == PASSES[0]), stop=(j == 1 and (a, b) == PASSES[-1]))
                    ins.then_inc(s_d, 1)

            def body(c2):
                first = isinstance(c2, int)
                for m in range(8):
                    n = 8 * c2 + m
                    up(n, c2, m)
                    if first and m < 3:
                        turn(m + 1)
                    if m:
                        down(n - 1, c2, m - 1)
                    elif not first:
                        down(n - 1, c2 - 1, 7)
            turn(0)
            body(0)
            with pe.Fori(1, NC // 2) as c2:
                body(c2)
            down(4 * NC - 1, NC // 2 - 1, 7)

        @block.scalar
        def _(act):
            def turn(g):
                for i in range(TPG):
                    t = TPG * g + i
                    act.wait_ge(s_tr, t + 1)
                    act.copy(xT[:, 0, :, t * P:(t + 1) * P], T[i % 2][:].rearrange("p (k n) -> p k n", k=KH)).then_inc(s_xhi, 1)

            def body(c2):
                first = isinstance(c2, int)
                for m in range(8):
                    n, p = 8 * c2 + m, m // 4
                    if m % 4 == 0:
                        act.wait_ge(s_wu[p], 32 * c2 + 32)
                    for j in range(2):
                        act.wait_ge(s_u, 4 * n + j + 1)
                        wait(act, s_h, 2 * n - 1 + j)
                        act.activation(sil[:, j, :], U[j][:], ACT.Silu, scale=sc[p][:, j:j + 1]).then_inc(s_sil, 1)
                    for j in range(2):
                        act.wait_ge(s_h, 2 * n + j + 1)
                        wait(act, s_d, 4 * n - 4)
                        act.copy(hb[:, m % 2, 0, j, :], hf[:, j, :]).then_inc(s_hi, 1)
                    if first and m < 3:
                        turn(m + 1)
            turn(0)
            body(0)
            with act.Fori(1, NC // 2) as c2:
                body(c2)

        @block.vector
        def _(dve):
            own = Chain(dve, s_own)

            def rows(g):
                def free(i):
                    wait(dve, s_tr, TPG * (g - 1) + i + 1)
                    return s_xn
                wait(dve, s_xn, TPG * g)
                normalize(dve, st, mv, xn, [res[:, TPG * g + i, :] for i in range(TPG)], own, free)

            def turn(g):
                for i in range(TPG):
                    t = TPG * g + i
                    dve.wait_ge(s_xhi, t + 1)
                    at = slice(t * P, (t + 1) * P)
                    dve.tensor_tensor(xT[:, 1, :, at], T[i % 2][:].rearrange("p (k n) -> p k n", k=KH),
                                      xT[:, 0, :, at].bitcast(F32), ALU.subtract).then_inc(s_xlo, 1)

            def add(n, m):
                for t in range(TPG):
                    dve.wait_ge(s_d, 4 * n + t + 1)
                    r = res[:, TPG * (m % 4) + t, :]
                    dve.tensor_tensor(r, D[t % 2][:], r, ALU.add).then_inc(s_acc, 1)

            def body(c2):
                first = isinstance(c2, int)
                for m in range(8):
                    n, p = 8 * c2 + m, m // 4
                    if first and m < 3:
                        rows(m + 1)
                    if m % 4 == 0:
                        dve.wait_ge(s_wu[p], 32 * c2 + 32)
                    for j in range(2):
                        dve.wait_ge(s_sil, 2 * n + j + 1)
                        dve.wait_ge(s_u, 4 * n + j + 3)
                        wait(dve, s_hi, 2 * n - 1 + j)
                        wait(dve, s_lo, 2 * n - 1 + j)
                        dve.scalar_tensor_tensor(hf[:, j, :], U[2 + j][:], sc[p][:, 2 + j:3 + j], sil[:, j, :],
                                                 ALU.mult, ALU.mult).then_inc(s_h, 1)
                    for j in range(2):
                        dve.wait_ge(s_hi, 2 * n + j + 1)
                        dve.tensor_tensor(hb[:, m % 2, 1, j, :], hf[:, j, :], hb[:, m % 2, 0, j, :].bitcast(F32),
                                          ALU.subtract).then_inc(s_lo, 1)
                    if first and m < 3:
                        turn(m + 1)
                    if not (first and m == 0):
                        add(n - 1, (m - 1) % 8)
            rows(0)
            turn(0)
            body(0)
            with dve.Fori(1, NC // 2) as c2:
                body(c2)
            add(4 * NC - 1, 7)


def mixer(nc, s, in_s, out_s):
    res, cs, pr, banks, i2r, ones = s["res"], s["cs"], s["pr"], s["banks"], s["i2r"], s["ones"]
    RING = 4
    NLOAD = NIN + NB
    NIP = NLOAD - 1
    LCONV = 2 + NB
    POOL_M = {0: (3,), 1: (2, 3)}
    with ExitStack() as ctx:
        def sb(name, shape, dt=F32):
            return ctx.enter_context(nc.sbuf_tensor(f"m_{name}", shape, dt))

        def sem(name):
            return ctx.enter_context(nc.semaphore(f"ms_{name}"))

        xn, st, mv = sb("xn", [P, TPG, HID]), sb("st", [P, TPG, 6]), sb("mv", [P, 4, TPG])
        xT = sb("xT", [P, 2, KH, SEQ], F32R)
        ring = [sb(f"w{i}", [P, 2, HID], F32R) for i in range(RING)]
        xr = sb("xr", [P, 2, SEQ + 4])
        cv = sb("cv", [P, 2, SEQ])
        xc, zs = sb("xc", [P, 2, SEQ]), sb("zs", [P, 2, SEQ])
        Bf, Cf = sb("Bf", [P, SEQ]), sb("Cf", [P, SEQ])
        du, de, dw, dl, dtf = (sb(n, [P, SEQ]) for n in ("du", "de", "dw", "dl", "dtf"))
        da = sb("da", [P, SEQ])
        ec = sb("ec", [P, SEQ])
        aS, eS = sb("aS", [P, SEQ], F32R), sb("eS", [P, SEQ], F32R)
        dg = sb("dg", [HEADS, 2, HEADS])
        GT = sb("GT", [P, SEQ])
        Bt = sb("Bt", [P, 3, STATE])
        dd = sb("dd", [P, 6 * HEADS])
        xp = sb("xp", [P, 2, NCK, HPB, 32])
        L = sb("L", [P, 2, 4, SEQ])
        xd = sb("xd", [P, 2, 3, P])
        sta = sb("sta", [P, 2, 3, P])
        ex, z, y = sb("ex", [P, 2, SEQ]), sb("z", [P, 2, SEQ]), sb("y", [P, 2, SEQ])
        yh = sb("yh", [P, NB, 2, SEQ], F32R)
        sq, ss = sb("sq", [P, SEQ]), sb("ss", [P, SEQ])
        rr = sb("rr", [P, 3 * TPG])
        i2x = sb("i2x", [P, INTER], F32R)
        (s_xn, s_tr, s_xhi, s_xlo, s_ip, s_pev, s_raw, s_cv, s_xcv, s_zs, s_u, s_e, s_ln, s_a, s_ah, s_eh,
         s_nu, s_dw, s_dt, s_as, s_ec, s_es, s_dg, s_G, s_B, s_D, s_gt, s_bt, s_dd, s_X, s_xp, s_A, s_sc,
         s_xd, s_mv, s_mp, s_Y, s_S, s_st, s_O, s_E, s_ex, s_y, s_z, s_yf, s_ss, s_yh, s_yl, s_V, s_v,
         s_op, s_fin, s_own, s_po, s_z0) = (sem(n) for n in (
             "xn tr xhi xlo ip pev raw cv xcv zs u e ln a ah eh nu dw dt as ec es dg G B D gt bt dd X xp A sc "
             "xd mv mp Y S st O E ex y z yf ss yh yl V v op fin own po z0").split())
        s_w = [sem(f"w{i}") for i in range(RING)]
        PB, A, Y, X, S, O = banks[0:2], banks[2:4], banks[4], banks[5], banks[6], banks[7]
        OUT = [A[0], A[1], S, O]
        I = cs[:, C_I4:C_I4 + P]
        order = [BI_DT, BI_B, BI_C] + [i for b in range(NB) for i in (NB + b, b)]

        def loads(slot):
            return len(range(slot, NLOAD, RING))

        def ck(c):
            return slice(c * P, (c + 1) * P)

        block = ctx.enter_context(nc.Block())

        def over_sequences(eng, body):
            body(0)
            with eng.Fori(1, BATCH) as q:
                body(q)

        @block.sync
        def _(sp):
            def body(q):
                for n in range(NLOAD):
                    if n < RING:
                        wait(sp, s_op, TPG * q)
                    else:
                        wait(sp, s_ip, NIP * q + n - RING + 1)
                    src = in_s[order[n]] if n < NIN else out_s[n - NIN]
                    sp.dma_start(ring[n % RING][:].rearrange("p h n -> p (h n)").bitcast(F32), src).then_inc(s_w[n % RING], 16)
            over_sequences(sp, body)

        @block.tensor
        def _(pe):
            def body(q):
                def landed(n):
                    wait(pe, s_w[n % RING], 16 * (loads(n % RING) * q + n // RING + 1))

                def in_proj(n):
                    w = ring[n % RING][:].rearrange("p h (k m) -> p h k m", k=KH)
                    for k in range(KH):
                        for i, (a, b) in enumerate(PASSES):
                            if k == 0 and i == 0:
                                landed(n)
                                wait(pe, s_pev, NIN * q + n - 1 if n >= 2 else NIN * q)
                            ins = pe.matmul(PB[n % 2][:], w[:, a, k, :], xT[:, b, k, :],
                                            start=(k == 0 and i == 0), stop=(k == KH - 1 and i == 2))
                            if k == KH - 1 and i == 2:
                                ins.then_inc(s_ip, 1)
                            yield

                def run(gen):
                    for _ in gen:
                        pass

                def ydiag(qd):
                    b, e = qd // 2, qd % 2
                    if e == 0:
                        wait(pe, s_y, NB * q + b)
                        if b == 0:
                            wait(pe, s_v, q)
                    pe.wait_ge(s_xp, NB * q + b + 1)
                    pe.wait_ge(s_mv, 2 * NB * q + qd + 1)
                    pe.wait_ge(s_mp, 2 * NB * q + qd + 1)
                    for c in range(NCK):
                        for j in range(4):
                            ins = pe.matmul(Y[32 * j:32 * j + 32, ck(c)], xp[:, b % 2, c, 2 * j + e, :], L[:, e, j, ck(c)],
                                            start=(e == 0 and c == 0), stop=(e == 1), skip_group_check=True)
                    ins.then_inc(s_Y, 1)

                def tail(b):
                    if b < NB - 1:
                        pe.wait_ge(s_xp, NB * q + b + 2)
                    else:
                        pe.wait_ge(s_ex, NB * q + b)
                    if b == 0:
                        pe.wait_ge(s_es, q + 1)
                    pe.matmul(X[:], i2x[:, ck(b)], eS[:],
                              start=True, stop=True).then_inc(s_E, 1)
                    pe.wait_ge(s_xd, 2 * (NB * q + b + 1))
                    if b:
                        pe.wait_ge(s_st, NB * q + b)
                    else:
                        pe.wait_ge(s_gt, q + 1)
                        pe.wait_ge(s_bt, q + 1)
                    for c in range(3):
                        ins = pe.matmul(S[:, ck(c)], Bt[:, c, :], xd[:, b % 2, c, :], start=True, stop=True)
                    ins.then_inc(s_S, 1)
                    ydiag(2 * b + 1)
                    pe.wait_ge(s_st, NB * q + b + 1)
                    wait(pe, s_z, NB * q + b)
                    for c in range(1, NCK):
                        ins = pe.matmul(O[:, ck(c)], sta[:, b % 2, c - 1, :], Cf[:, ck(c)], start=True, stop=True)
                    ins.then_inc(s_O, 1)

                for i in range(TPG):
                    pe.wait_ge(s_xn, TPG * q + i + 1)
                    wait(pe, s_xlo, TPG * q + i - 1)
                    wait(pe, s_fin, TPG * q)
                    for k in range(KH):
                        ins = pe.transpose(A[i % 2][:, ck(k)], xn[:, i, ck(k)], I)
                    ins.then_inc(s_tr, 1)
                pe.wait_ge(s_xlo, TPG * (q + 1))
                for n in range(5):
                    run(in_proj(n))
                pe.wait_ge(s_xcv, LCONV * q + 2)
                for c in range(NCK):
                    ins = pe.matmul(S[:, ck(c)], Bf[:, ck(c)], Cf[:, ck(c)], start=True, stop=True)
                ins.then_inc(s_G, 1)
                for c in range(3):
                    ins = pe.transpose(O[:, ck(c)], Bf[:, ck(c)], I)
                ins.then_inc(s_B, 1)
                pe.wait_ge(s_dt, q + 1)
                wait(pe, s_ex, NB * q)
                pe.wait_ge(s_dg, q + 1)
                for i in range(2):
                    pe.matmul(X[:, HEADS * (4 + i):HEADS * (5 + i)], ones[0:HEADS, :], dg[:, i, :], start=True, stop=True)
                for c in range(NCK):
                    ins = pe.transpose(X[:, HEADS * c:HEADS * (c + 1)], dtf[0:HEADS, ck(c)], cs[0:HEADS, C_I4:C_I4 + HEADS])
                ins.then_inc(s_D, 1)
                for b in range(NB):
                    pe.wait_ge(s_xcv, LCONV * q + 2 + b + 1)
                    if b == 0:
                        pe.wait_ge(s_dd, q + 1)
                    elif b == 1:
                        pe.wait_ge(s_xp, NB * q + 1)
                    else:
                        pe.wait_ge(s_ex, NB * q + b - 1)
                    for c in range(NCK):
                        ins = pe.transpose(X[:, ck(c)], xc[:, b % 2, ck(c)], I)
                    ins.then_inc(s_X, 1)
                    for e in range(2):
                        fill = in_proj(5 + 2 * b + e) if b < NB - 1 else iter(())
                        for j in range(4):
                            n = 8 * b + 4 * e + j
                            if n == 0:
                                pe.wait_ge(s_as, q + 1)
                            wait(pe, s_sc, 64 * q + n - 1)
                            h = HPB * b + 2 * j + e
                            pe.matmul(A[n % 2][:], i2r[:, h:h + 1].to_broadcast([P, P]), aS[:], start=True, stop=True).then_inc(s_A, 1)
                            for _ in range(3):
                                next(fill, None)
                        if e == 1:
                            ydiag(2 * b)
                        elif b:
                            tail(b - 1)
                tail(NB - 1)
                pe.wait_ge(s_ss, NB * (q + 1))
                pe.wait_ge(s_y, NB * (q + 1))
                for t in range(TPG):
                    ins = pe.matmul(Y[:, t:t + 1], ss[:, ck(t)], ones[:, 0:1], start=True, stop=True)
                ins.then_inc(s_V, 1)
                pe.wait_ge(s_sc, 64 * (q + 1))
                pe.wait_ge(s_z, NB * (q + 1))
                for b in range(NB):
                    landed(NIN + b)
                    pe.wait_ge(s_yl, NB * q + b + 1)
                    for t in range(TPG):
                        for i, (m, n) in enumerate(PASSES):
                            ins = pe.matmul(OUT[t][:], yh[:, b, m, ck(t)], ring[(NIN + b) % RING][:, n, :],
                                            start=(b == 0 and i == 0), stop=(b == NB - 1 and i == 2))
                        if b == NB - 1:
                            ins.then_inc(s_op, 1)
                    if b < NB - 1:
                        ins.then_inc(s_ip, 1)
            over_sequences(pe, body)

        @block.scalar
        def _(act):
            def body(q):
                def raw(n, col):
                    at = (1, 2)[n] if n < 2 else 3 + 2 * (n - 2)
                    act.wait_ge(s_ip, NIP * q + at + 1)
                    wait(act, s_cv, LCONV * q + n - 1)
                    wait(act, s_xcv, LCONV * q + n - 1)
                    act.copy(xr[:, n % 2, 3:3 + SEQ], PB[at % 2][:])
                    w = P_CW + 4 * col
                    act.activation(cv[:, n % 2, :], PB[at % 2][:], ACT.Identity, scale=pr[:, w + 3:w + 4],
                                   bias=pr[:, P_CB + col:P_CB + col + 1]).then_inc(s_pev, 1)

                def conv_silu(n, dst):
                    act.wait_ge(s_cv, LCONV * q + n + 1)
                    act.activation(dst, cv[:, n % 2, :], ACT.Silu).then_inc(s_xcv, 1)

                def x_silu(b):
                    wait(act, s_X, NB * q + b - 1)
                    wait(act, s_y, NB * q + b - 1)
                    conv_silu(2 + b, xc[:, b % 2, :])

                def gate(b):
                    act.wait_ge(s_ip, NIP * q + 5 + 2 * b)
                    wait(act, s_yf, NB * q + b - 1)
                    act.activation(zs[:, b % 2, :], PB[(4 + 2 * b) % 2][:], ACT.Silu).then_inc(s_pev, 1)

                for i in range(TPG):
                    act.wait_ge(s_tr, TPG * q + i + 1)
                    wait(act, s_ip, NIP * q - (NB - 1))
                    act.copy(xT[:, 0, :, ck(i)], A[i % 2][:].rearrange("p (k n) -> p k n", k=KH)).then_inc(s_xhi, 1)
                act.wait_ge(s_ip, NIP * q + 1)
                wait(act, s_dt, q)
                act.activation(du[:], PB[0][:], ACT.Identity, bias=pr[:, P_DTB:P_DTB + 1]).then_inc(s_pev, 1)
                raw(0, NB)
                act.wait_ge(s_nu, q + 1)
                act.activation(de[:], de[:], ACT.Exp).then_inc(s_e, 1)
                raw(1, NB + 1)
                act.wait_ge(s_dw, q + 1)
                act.activation(dl[:], dw[:], ACT.Ln).then_inc(s_ln, 1)
                act.wait_ge(s_dt, q + 1)
                wait(act, s_as, q)
                act.activation(da[:], dtf[:], ACT.Exp, scale=s["acol"][:, 0:1]).then_inc(s_a, 1)
                act.wait_ge(s_a, q + 1)
                wait(act, s_A, 64 * q)
                act.copy(aS[:], da[:]).then_inc(s_ah, 1)
                wait(act, s_O, NB * q)
                conv_silu(0, Bf[:])
                conv_silu(1, Cf[:])
                raw(2, 0)
                gate(0)
                x_silu(0)
                act.wait_ge(s_ec, q + 1)
                wait(act, s_E, NB * q)
                act.copy(eS[:], ec[:]).then_inc(s_eh, 1)
                act.wait_ge(s_B, q + 1)
                act.copy(Bt[:].rearrange("p c n -> p (c n)"), O[:, 0:3 * P]).then_inc(s_bt, 1)

                def tail(b):
                    act.wait_ge(s_E, NB * q + b + 1)
                    wait(act, s_z, NB * q + b - 1)
                    act.copy(ex[:, b % 2, :], X[:]).then_inc(s_ex, 1)
                    act.wait_ge(s_yf, NB * q + b + 1)
                    wait(act, s_op, TPG * q)
                    act.copy(yh[:, b, 0, :], y[:, b % 2, :]).then_inc(s_yh, 1)

                for b in range(NB):
                    if b < NB - 1:
                        raw(3 + b, b + 1)
                    if b:
                        tail(b - 1)
                    if b < NB - 1:
                        x_silu(b + 1)
                        gate(b + 1)
                tail(NB - 1)
            over_sequences(act, body)

        @block.vector
        def _(dve):
            own_n = [0]

            dve.memset(xp[:], 0.0).then_inc(s_z0, 1)
            dve.memset(xr[:, :, 0:3], 0.0).then_inc(s_z0, 1)
            dve.tensor_copy(i2x[:].rearrange("p (h d) -> p h d", d=HDIM),
                            cs[:, C_I2:C_I2 + HEADS].unsqueeze(2).to_broadcast([P, HEADS, HDIM])).then_inc(s_z0, 1)
            dve.wait_ge(s_z0, 3)

            def body(q):
                per_q = own_n[0] if not isinstance(q, int) else 0
                own = Chain(dve, s_own, per_q * q)

                def conv(n, col):
                    dve.wait_ge(s_pev, NIN * q + ((1, 2)[n] if n < 2 else 3 + 2 * (n - 2)) + 1)
                    w = P_CW + 4 * col
                    for k in range(3):
                        ins = dve.scalar_tensor_tensor(cv[:, n % 2, :], xr[:, n % 2, k:k + SEQ], pr[:, w + k:w + k + 1],
                                                       cv[:, n % 2, :], ALU.mult, ALU.add)
                        if k < 2:
                            own.step(ins)
                    ins.then_inc(s_cv, 1)

                def quad_scans(qd):
                    for j in range(4):
                        n = 4 * qd + j
                        dve.wait_ge(s_A, 64 * q + n + 1)
                        wait(dve, s_Y, 2 * NB * q + qd - 1)
                        dve.tensor_tensor_scan(L[:, qd % 2, j, :], A[n % 2][:], cs[:, C_I4:C_I4 + SEQ], 0.0,
                                               ALU.mult, ALU.add).then_inc(s_sc, 1)

                def padded(b):
                    dve.wait_ge(s_X, NB * q + b + 1)
                    wait(dve, s_Y, 2 * (NB * q + b - 1))
                    xv = X[:].rearrange("p (c j e d) -> p c j e d", c=NCK, j=4, e=2)
                    dv = dd[:, 0:NCK * HEADS].rearrange("p (c h) -> p c h", c=NCK)
                    pv = xp[:, b % 2].rearrange("p c (j e) m -> p c j e m", e=2)
                    for e in range(2):
                        dt = dv[:, :, HPB * b + e:HPB * (b + 1):2].unsqueeze(3).to_broadcast([P, NCK, 4, HDIM])
                        ins = dve.tensor_tensor(pv[:, :, :, e, HDIM * e:HDIM * (e + 1)], xv[:, :, :, e, :], dt, ALU.mult)
                    ins.then_inc(s_xp, 1)

                def decayed(qd):
                    b, e = qd // 2, qd % 2
                    dve.wait_ge(s_sc, 64 * q + 4 * qd + 4)
                    dve.wait_ge(s_xp, NB * q + b + 1)
                    wait(dve, s_S, NB * q + b - 1)
                    pv = xp[:, b % 2].rearrange("p c (j e) m -> p c j e m", e=2)[:, 0:3, :, e, HDIM * e:HDIM * (e + 1)]
                    last = L[:, e].rearrange("p j (c l) -> p c j l", c=NCK)[:, 0:3, :, P - 1:P].to_broadcast([P, 3, 4, HDIM])
                    out = xd[:, b % 2].rearrange("p c (j e d) -> p c j e d", j=4, e=2)[:, :, :, e, :]
                    dve.tensor_tensor(out, pv, last, ALU.mult).then_inc(s_xd, 1)

                def times_g(qd):
                    e = qd % 2
                    dve.wait_ge(s_xd, 2 * NB * q + qd + 1)
                    for j in range(4):
                        if j not in POOL_M[e]:
                            ins = dve.tensor_tensor(L[:, e, j, :], L[:, e, j, :], GT[:], ALU.mult)
                    ins.then_inc(s_mv, 1)

                def states(b):
                    dve.wait_ge(s_S, NB * q + b + 1)
                    wait(dve, s_O, NB * q + b - 1)
                    own.step(dve.tensor_copy(sta[:, b % 2, 0, :], S[:, ck(0)]))
                    for i in range(2):
                        at = HEADS * (4 + i) + HPB * b
                        decay = dd[:, at:at + HPB].unsqueeze(2).to_broadcast([P, HPB, HDIM])
                        own.step(dve.tensor_tensor(sta[:, b % 2, i + 1, :].rearrange("p (h d) -> p h d", h=HPB),
                                                   sta[:, b % 2, i, :].rearrange("p (h d) -> p h d", h=HPB), decay, ALU.mult))
                        ins = dve.tensor_tensor(sta[:, b % 2, i + 1, :], S[:, ck(i + 1)], sta[:, b % 2, i + 1, :], ALU.add)
                        if i == 0:
                            own.step(ins)
                    ins.then_inc(s_st, 1)

                def combine(b):
                    dve.wait_ge(s_Y, 2 * (NB * q + b + 1))
                    wait(dve, s_ss, NB * q + b - 1)
                    wait(dve, s_yh, NB * q + b - 1)
                    wait(dve, s_yl, NB * q + b - 1)
                    dve.scalar_tensor_tensor(y[:, b % 2, :], xc[:, b % 2, :], pr[:, P_D + b:P_D + b + 1], Y[:],
                                             ALU.mult, ALU.add).then_inc(s_y, 1)
                    dve.wait_ge(s_O, NB * q + b + 1)
                    dve.wait_ge(s_ex, NB * q + b + 1)
                    dve.tensor_tensor(z[:, b % 2, P:SEQ], O[:, P:SEQ], ex[:, b % 2, P:SEQ], ALU.mult).then_inc(s_z, 1)

                def low(b):
                    dve.wait_ge(s_yh, NB * q + b + 1)
                    dve.tensor_tensor(yh[:, b, 1, :], y[:, b % 2, :], yh[:, b, 0, :].bitcast(F32), ALU.subtract).then_inc(s_yl, 1)

                def free(i):
                    wait(dve, s_tr, TPG * (q - 1) + i + 1)
                    return s_xn
                wait(dve, s_xn, TPG * q)
                wait(dve, s_fin, TPG * q)
                tile = [res[:, bass.ds(TPG * q + i, 1), :].rearrange("p o n -> p (o n)") for i in range(TPG)]
                normalize(dve, st, mv, xn, tile, own, free)
                for i in range(TPG):
                    dve.wait_ge(s_xhi, TPG * q + i + 1)
                    dve.tensor_tensor(xT[:, 1, :, ck(i)], A[i % 2][:].rearrange("p (k n) -> p k n", k=KH),
                                      xT[:, 0, :, ck(i)].bitcast(F32), ALU.subtract).then_inc(s_xlo, 1)
                dve.wait_ge(s_pev, NIN * q + 1)
                wait(dve, s_es, q)
                dve.scalar_tensor_tensor(de[:], du[:], -1.0, du[:], ALU.mult, ALU.min).then_inc(s_nu, 1)
                conv(0, NB)
                dve.wait_ge(s_e, q + 1)
                dve.tensor_scalar(dw[:], de[:], 1.0, None, ALU.add).then_inc(s_dw, 1)
                conv(1, NB + 1)
                dve.wait_ge(s_dw, q + 1)
                own.step(dve.scalar_tensor_tensor(de[:], dw[:], -1.0, de[:], ALU.add, ALU.subtract))
                dve.wait_ge(s_ln, q + 1)
                own.step(dve.reciprocal(dw[:], dw[:]))
                own.step(dve.tensor_tensor(de[:], de[:], dw[:], ALU.mult))
                own.step(dve.tensor_tensor(dl[:], dl[:], de[:], ALU.subtract))
                own.step(dve.scalar_tensor_tensor(dl[:], du[:], 0.0, dl[:], ALU.max, ALU.add))
                wait(dve, s_D, q)
                dve.tensor_scalar(dtf[:], dl[:], 100.0, 0.0, ALU.min, ALU.max).then_inc(s_dt, 1)
                dve.wait_ge(s_a, q + 1)
                wait(dve, s_eh, q)
                for c in range(NCK):
                    ins = dve.tensor_tensor_scan(ec[:, ck(c)], da[:, ck(c)], ones[:], 1.0, ALU.mult, ALU.mult)
                ins.then_inc(s_ec, 1)
                dve.wait_ge(s_ah, q + 1)
                own.step(dve.tensor_tensor(aS[HEADS:P, :], da[HEADS:P, :], aS[HEADS:P, :].bitcast(F32), ALU.subtract))
                dve.memset(aS[:, 0:SEQ:P].bitcast(F32), 0.0).then_inc(s_as, 1)
                dve.wait_ge(s_ec, q + 1)
                for i in range(2):
                    at = (i + 2) * P - 1
                    ins = dve.tensor_scalar(dg[:, i, :], cs[0:HEADS, C_I2:C_I2 + HEADS], ec[0:HEADS, at:at + 1], None, ALU.mult)
                ins.then_inc(s_dg, 1)
                conv(2, 0)
                dve.wait_ge(s_eh, q + 1)
                dve.tensor_tensor(eS[HEADS:P, :], ec[HEADS:P, :], eS[HEADS:P, :].bitcast(F32), ALU.subtract).then_inc(s_es, 1)
                dve.wait_ge(s_G, q + 1)
                wait(dve, s_mp, 2 * NB * q)
                wait(dve, s_mv, 2 * NB * q)
                dve.tensor_copy(GT[:], S[:]).then_inc(s_gt, 1)
                dve.wait_ge(s_D, q + 1)
                wait(dve, s_st, NB * q)
                dve.tensor_copy(dd[:], X[:, 0:6 * HEADS]).then_inc(s_dd, 1)
                dve.wait_ge(s_gt, q + 1)
                dve.wait_ge(s_dd, q + 1)
                for b in range(NB):
                    for e in range(2):
                        quad_scans(2 * b + e)
                        if e == 0:
                            padded(b)
                            if b:
                                states(b - 1)
                        decayed(2 * b + e)
                        times_g(2 * b + e)
                        if e == 0 and b:
                            combine(b - 1)
                        if e == 1 and b < NB - 1:
                            conv(3 + b, b + 1)
                        if e == 1 and b:
                            low(b - 1)
                states(NB - 1)
                combine(NB - 1)
                low(NB - 1)
                dve.wait_ge(s_V, q + 1)
                dve.tensor_copy(rr[:, 0:TPG], Y[:, 0:TPG]).then_inc(s_v, 1)
                dve.wait_ge(s_v, q + 1)
                rsqrt(dve, own, rr[:, TPG:2 * TPG], rr[:, 0:TPG], rr[:, 2 * TPG:3 * TPG], 1.0 / INTER)
                for t in range(TPG):
                    dve.wait_ge(s_op, TPG * q + t + 1)
                    dve.scalar_tensor_tensor(tile[t], OUT[t][:], rr[:, TPG + t:TPG + t + 1], tile[t],
                                             ALU.mult, ALU.add).then_inc(s_fin, 1)
                own_n[0] = own.n
            over_sequences(dve, body)

        @block.gpsimd
        def _(pool):
            def body(q):
                own = Chain(pool, s_po, (2 * NB - 1) * q)

                def times_g(qd):
                    e = qd % 2
                    if qd == 0:
                        pool.wait_ge(s_gt, q + 1)
                    pool.wait_ge(s_xd, 2 * NB * q + qd + 1)
                    for j in POOL_M[e]:
                        ins = pool.tensor_tensor(L[:, e, j, :], L[:, e, j, :], GT[:], ALU.mult)
                    ins.then_inc(s_mp, 1)

                def combine(b):
                    pool.wait_ge(s_z, NB * q + b + 1)
                    v = y[:, b % 2, :]
                    own.step(pool.tensor_tensor(y[:, b % 2, P:SEQ], y[:, b % 2, P:SEQ], z[:, b % 2, P:SEQ], ALU.add))
                    gate_done = NIN * q + 5 + 2 * b
                    pool.wait_ge(s_pev, gate_done)
                    ins = pool.tensor_tensor(v, v, zs[:, b % 2, :], ALU.mult)
                    ins.then_inc(s_yf, 1)
                    pool.wait_ge(s_yf, NB * q + b + 1)
                    wait(pool, s_ss, NB * q + b)
                    if b == 0:
                        wait(pool, s_V, q)
                        pool.tensor_tensor(ss[:], v, v, ALU.mult).then_inc(s_ss, 1)
                    else:
                        own.step(pool.tensor_tensor(sq[:], v, v, ALU.mult))
                        pool.tensor_tensor(ss[:], ss[:], sq[:], ALU.add).then_inc(s_ss, 1)

                for b in range(NB):
                    for e in range(2):
                        times_g(2 * b + e)
                        if e == 0 and b:
                            combine(b - 1)
                combine(NB - 1)
            over_sequences(pool, body)



def kernel(**inputs):
    import concourse.bacc as _bacc
    from concourse.bass_utils import run_bass_kernel_spmd as _run

    I = {k.split("_", 1)[1]: np.asarray(v) for k, v in inputs.items()}
    f = np.float32

    def cols(v):
        return np.ascontiguousarray(v.reshape(-1, P).T)

    def rows(wT):
        K, N = wT.shape
        return wT.reshape(K // P, P, N).transpose(1, 0, 2).reshape(P, -1)

    gate, up = I["ffn_W_gate"], I["ffn_W_up"]
    wug = np.stack([rows(np.concatenate([w[c * CH:(c + 1) * CH] for w in (gate, up)]).T) for c in range(NC)])
    sc = I["ffn_Wscale_ug"]
    wsc = np.stack([np.concatenate([cols(sc[o + c * CH:o + (c + 1) * CH]) for o in (FF, 0)], 1) for c in range(NC)])
    wdn = rows(I["ffn_W_down"].T)
    w = I["attn_in_proj_w"]
    w = np.concatenate([w, w[-HEADS:], np.zeros((P, HID), f)])
    win = np.stack([rows(w[b * P:(b + 1) * P].T) for b in range(NIN + 1)])
    wout = I["attn_out_proj_w"].T.reshape(NB, P, HID)
    had = np.ones((1, 1), f)
    while had.shape[0] < P:
        had = np.block([[had, had], [had, -had]])
    eye = np.eye(P, dtype=f)
    cst = np.concatenate([had, np.tile(eye, (1, 4)), np.tile(np.eye(HEADS, dtype=f), (2, 1))], 1)
    par = np.concatenate([
        cols(I["ffn_SU_ug"]), cols(I["ffn_SU_dp"]),
        np.tile(I["attn_A_log"], 2)[:, None], np.tile(I["attn_dt_bias"], 2)[:, None],
        cols(np.repeat(I["attn_D"], HDIM)),
        I["attn_conv_w"].reshape(10, P, 4).transpose(1, 0, 2).reshape(P, 40), cols(I["attn_conv_b"]),
        cols(I["attn_norm_w"]), np.broadcast_to(I["ffn_Wscale_dp"], (P, HID))], 1)
    arrays = dict(x=I["attn_hidden_states"].reshape(TOK, HID), wug=wug, wsc=wsc, wdn=wdn, win=win, wout=wout, cst=cst, par=par)

    nc = _bacc.Bacc("TRN2", target_bir_lowering=False, num_devices=1)
    arrays = {f"in_{k}": np.ascontiguousarray(v) for k, v in arrays.items()}
    args = [nc.dram_tensor(k, v.shape, F32, kind="ExternalInput").ap() for k, v in arrays.items()]
    args.append(nc.dram_tensor("out", (TOK, HID), F32, kind="ExternalOutput").ap())
    program(nc, *args)
    r = _run(nc, [arrays], core_ids=[0])
    return r.results[0]["out"].reshape(BATCH, SEQ, HID)
```

```python
from contextlib import ExitStack
import math

import numpy as np
import concourse.bass as bass
from concourse import mybir

F32 = mybir.dt.float32
F32R = mybir.dt.float32r
ALU = mybir.AluOpType
ACT = mybir.ActivationFunctionType

P = 128
BATCH, SEQ, HID = 4, 512, 512
TOK = BATCH * SEQ
NT = TOK // P
KH = HID // P
FF = 2048
CH = 256
NC = FF // CH
FB = FF // P
G = TOK // 512
TPG = 512 // P
INTER, STATE, HEADS, HDIM = 1024, 128, 64, 16
NB = INTER // P
HPB = P // HDIM
NIN = 2 * NB + 3
BI_B, BI_C, BI_DT = 2 * NB, 2 * NB + 1, 2 * NB + 2
NCK = SEQ // P
EPS = 1e-5

C_H, C_I4, C_I2, C_END = 0, P, P + 4 * P, P + 4 * P + HEADS
_c = np.cumsum([0, KH, FB, 1, 1, NB, 40, 10, NB, HID]).tolist()
P_SUG, P_SUD, P_ALOG, P_DTB, P_D, P_CW, P_CB, P_NW, P_WDP, P_END = _c

PASSES = ((0, 0), (0, 1), (1, 0))


def wait(eng, sem, value):
    if isinstance(value, int) and value <= 0:
        return
    eng.wait_ge(sem, value)


def run(steps):
    for _ in steps:
        pass


class Chain:

    def __init__(self, eng, sem, base=0):
        self.eng, self.sem, self.n, self.base = eng, sem, 0, base

    def done(self, ins):
        self.n += 1
        ins.then_inc(self.sem, 1)

    def sync(self):
        wait(self.eng, self.sem, self.base + self.n)

    def step(self, ins):
        self.done(ins)
        self.sync()


def program(nc, x, wug, wsc, wdn, win, wout, cst, par, out):
    ug_s = nc.dram_tensor("ug_split", [NC, P, 2 * KH * 2 * CH], F32, kind="Internal").ap()
    dn_s = nc.dram_tensor("dn_split", [NC, P, 2 * 2 * HID], F32, kind="Internal").ap()
    in_s = nc.dram_tensor("in_split", [NIN + 1, P, 2 * HID], F32, kind="Internal").ap()
    out_s = nc.dram_tensor("out_split", [NB, P, 2 * HID], F32, kind="Internal").ap()
    with ExitStack() as ctx:
        res = ctx.enter_context(nc.sbuf_tensor("res", [P, NT, HID], F32))
        cs = ctx.enter_context(nc.sbuf_tensor("cs", [P, C_END], F32))
        pr = ctx.enter_context(nc.sbuf_tensor("pr", [P, P_END], F32))
        sug = ctx.enter_context(nc.sbuf_tensor("sug", [P, KH], F32))
        sud = ctx.enter_context(nc.sbuf_tensor("sud", [P, FB], F32))
        acol = ctx.enter_context(nc.sbuf_tensor("acol", [P, 1], F32))
        i2r = ctx.enter_context(nc.sbuf_tensor("i2r", [P, HEADS], F32R))
        ones = ctx.enter_context(nc.sbuf_tensor("ones", [P, P], F32))
        banks = [ctx.enter_context(nc.psum_tensor(f"bank{i}", [P, 512], F32)) for i in range(8)]
        s = dict(res=res, cs=cs, pr=pr, sug=sug, sud=sud, acol=acol, i2r=i2r, ones=ones, banks=banks)
        prepare(nc, s, x, wug, wdn, win, wout, cst, par, ug_s, dn_s, in_s, out_s)
        ffn(nc, s, "a", ug_s, dn_s, wsc)
        mixer(nc, s, in_s, out_s)
        ffn(nc, s, "b", ug_s, dn_s, wsc)
        store(nc, s, out)


def store(nc, s, out):
    with ExitStack() as ctx:
        s_out = ctx.enter_context(nc.semaphore("st_out"))
        block = ctx.enter_context(nc.Block())

        @block.sync
        def _(sp):
            sp.dma_start(out.rearrange("(t p) n -> p t n", p=P), s["res"][:]).then_inc(s_out, 16)
            sp.wait_ge(s_out, 16)


def prepare(nc, s, x, wug, wdn, win, wout, cst, par, ug_s, dn_s, in_s, out_s):
    res, cs, pr, banks = s["res"], s["cs"], s["pr"], s["banks"]
    with ExitStack() as ctx:
        def sb(name, shape, dt=F32):
            return ctx.enter_context(nc.sbuf_tensor(name, shape, dt))

        def sem(name):
            return ctx.enter_context(nc.semaphore(name))

        raw = sb("p_raw", [P, 2, KH, 512])
        t1 = sb("p_t1", [P, 2, KH, 512])
        t2 = sb("p_t2", [P, 2, KH, 512])
        wo = sb("p_wo", [P, 2, 2, KH, 512], F32R)
        da = sb("p_da", [P, FB, HID])
        db = sb("p_db", [P, FB, HID])
        sc = sb("p_sc", [P, 2, HID])
        s_par, s_x, s_d = sem("p_par"), sem("p_x"), sem("p_d")
        s_raw = [sem("p_raw0"), sem("p_raw1")]
        s_t1, s_t2, s_mm, s_hi, s_lo = sem("p_t1s"), sem("p_t2s"), sem("p_mm"), sem("p_hi"), sem("p_lo")
        s_st = [sem("p_st0"), sem("p_st1")]
        s_c, s_bf, s_dm, s_dsc, s_dhi, s_dlo = (sem(f"p_{n}") for n in ("c", "bf", "dm", "dsc", "dhi", "dlo"))
        s_ex, s_chi, s_clo = sem("p_ex"), sem("p_chi"), sem("p_clo")
        H = cs[:, C_H:C_H + P]
        NP = 7
        STAGES = FB.bit_length() - 1
        QD = FB // 4
        block = ctx.enter_context(nc.Block())

        def stored(eng, piece):
            wait(eng, s_st[piece % 2], 16 * (piece // 2 + 1) if piece >= 0 else 0)

        def ext(i):
            return (win if i < 5 else wout), (in_s if i < 5 else out_s), (i if i < 5 else i - 5)

        def put_ext(sp, i):
            piece = NC + i
            _, dst, at = ext(i)
            sp.dma_start(dst[4 * at:4 * at + 4].rearrange("b p (h n) -> p h b n", h=2),
                         wo[:, piece % 2].bitcast(F32)).then_inc(s_st[piece % 2], 16)

        def down_stored(eng, q):
            piece = NC + NP + q
            par_ = piece % 2
            before = (piece - 2) // 2 + 1 if q < 2 else (NC + NP + 1 - par_) // 2 + 2 * (q // 2)
            wait(eng, s_st[par_], 16 * before)

        @block.sync
        def _(sp):
            sp.dma_start(cs[:], cst).then_inc(s_par, 16)
            sp.dma_start(pr[:], par).then_inc(s_par, 16)
            for c in range(NC):
                wait(sp, s_t1, 2 * (c - 1))
                sp.dma_start(raw[:, c % 2], wug[c].rearrange("p (k n) -> p k n", k=KH)).then_inc(s_raw[c % 2], 16)
                if c == 0:
                    sp.dma_start(da[:], wdn.rearrange("p (k n) -> p k n", k=FB)).then_inc(s_d, 16)
                    sp.dma_start(res[:], x.rearrange("(t p) n -> p t n", p=P)).then_inc(s_x, 16)
                if c >= 2:
                    wait(sp, s_lo, KH * (c - 1))
                    sp.dma_start(ug_s[c - 2], wo[:, c % 2].rearrange("p h k n -> p (h k n)").bitcast(F32)).then_inc(s_st[c % 2], 16)
            for i in range(NP):
                piece = NC + i
                src, _, at = ext(i)
                if i < 2:
                    wait(sp, s_t1, 2 * (NC - 1 + i))
                else:
                    wait(sp, s_clo, i - 1)
                sp.dma_start(raw[:, piece % 2], src[4 * at:4 * at + 4].rearrange("b p n -> p b n")).then_inc(s_raw[piece % 2], 16)
                if i < 2:
                    wait(sp, s_lo, KH * (NC - 1 + i))
                    sp.dma_start(ug_s[NC - 2 + i], wo[:, piece % 2].rearrange("p h k n -> p (h k n)").bitcast(F32)).then_inc(s_st[piece % 2], 16)
                else:
                    put_ext(sp, i - 2)
            for i in (NP - 2, NP - 1):
                wait(sp, s_clo, i + 1)
                put_ext(sp, i)
            for q in range(QD):
                piece = NC + NP + q
                wait(sp, s_dlo, 4 * (q + 1))
                for h in range(2):
                    dst = dn_s[2 * q + h].rearrange("p (l j n) -> p l j n", l=2, j=2)
                    sp.dma_start(dst, wo[:, piece % 2, :, 2 * h:2 * h + 2, :].bitcast(F32)).then_inc(s_st[piece % 2], 16)
            sp.wait_ge(s_x, 16)
            total0 = 16 * (8 + 2 * 2)
            total1 = 16 * (7 + 2 * 2)
            sp.wait_ge(s_st[0], total0)
            sp.wait_ge(s_st[1], total1)

        @block.gpsimd
        def _(pool):
            for c in range(NC):
                wait(pool, s_raw[c % 2], 16 * (c // 2 + 1))
                wait(pool, s_t2, 2 * (c - 1))
                for n, op in enumerate((ALU.add, ALU.subtract)):
                    pool.tensor_tensor(t1[:, c % 2, n::2, :], raw[:, c % 2, 0::2, :], raw[:, c % 2, 1::2, :], op).then_inc(s_t1, 1)

        @block.tensor
        def _(pe):
            pe.wait_ge(s_par, 32)
            for c in range(NC):
                pe.wait_ge(s_t2, 2 * (c + 1))
                for k in range(KH):
                    wait(pe, s_lo, KH * (c - 2) + k + 1)
                    pe.matmul(banks[4 * (c % 2) + k][:], H, t2[:, c % 2, k, :], start=True, stop=True).then_inc(s_mm, 1)
            src = da if STAGES % 2 == 0 else db
            pe.wait_ge(s_bf, 2 * STAGES)
            for j in range(FB):
                if j < 8:
                    pe.wait_ge(s_lo, KH * (NC - 2) + j + 1)
                else:
                    pe.wait_ge(s_dsc, j - 7)
                pe.matmul(banks[j % 8][:], H, src[:, j, :], start=True, stop=True).then_inc(s_dm, 1)

        @block.scalar
        def _(act):
            act.wait_ge(s_par, 32)
            act.activation(s["acol"][:], pr[:, P_ALOG:P_ALOG + 1], ACT.Exp).then_inc(s_ex, 1)
            act.wait_ge(s_c, 4)
            for c in range(NC):
                stored(act, c - 2)
                for k in range(KH):
                    act.wait_ge(s_mm, KH * c + k + 1)
                    act.activation(wo[:, c % 2, 0, k, :], banks[4 * (c % 2) + k][:], ACT.Copy,
                                   scale=s["sug"][:, k:k + 1]).then_inc(s_hi, 1)
            for i in range(NP):
                piece = NC + i
                act.wait_ge(s_raw[piece % 2], 16 * (piece // 2 + 1))
                stored(act, piece - 2)
                for k in range(4):
                    scale = pr[:, P_NW + 4 * (i - 5) + k:P_NW + 4 * (i - 5) + k + 1] if i >= 5 else 1.0
                    act.activation(wo[:, piece % 2, 0, k, :], raw[:, piece % 2, k, :], ACT.Copy,
                                   scale=scale).then_inc(s_chi, 1)
            for j in range(FB):
                q = j // 4
                if j % 4 == 0:
                    down_stored(act, q)
                act.wait_ge(s_dsc, j + 1)
                act.copy(wo[:, (NC + NP + q) % 2, 0, j % 4, :], sc[:, j % 2, :]).then_inc(s_dhi, 1)

        @block.vector
        def _(dve):
            dve.memset(s["ones"][:], 1.0).then_inc(s_c, 1)
            dve.wait_ge(s_par, 32)
            dve.tensor_scalar(s["sug"][:], pr[:, P_SUG:P_SUG + KH], 1.0 / math.sqrt(HID), None, ALU.mult).then_inc(s_c, 1)
            dve.tensor_scalar(s["sud"][:], pr[:, P_SUD:P_SUD + FB], 0.5 / math.sqrt(FF), None, ALU.mult).then_inc(s_c, 1)
            dve.tensor_copy(s["i2r"][:], cs[:, C_I2:C_I2 + HEADS]).then_inc(s_c, 1)
            dve.wait_ge(s_ex, 1)
            dve.tensor_scalar(s["acol"][:], s["acol"][:], -1.0, None, ALU.mult).then_inc(s_c, 1)
            dve.wait_ge(s_c, 5)

            def butterfly(st):
                a, b = (da, db) if st % 2 == 0 else (db, da)
                w = 1 << st
                src = a[:].rearrange("p (u t w) n -> p u t (w n)", t=2, w=w)
                dst = b[:].rearrange("p (u t w) n -> p u t (w n)", t=2, w=w)
                wait(dve, s_bf, 2 * st)
                for t, op in enumerate((ALU.add, ALU.subtract)):
                    dve.tensor_tensor(dst[:, :, t, :], src[:, :, 0, :], src[:, :, 1, :], op).then_inc(s_bf, 1)

            dve.wait_ge(s_d, 16)
            for c in range(NC + 1):
                if c < NC:
                    dve.wait_ge(s_t1, 2 * (c + 1))
                    wait(dve, s_mm, KH * (c - 1))
                    for n, op in enumerate((ALU.add, ALU.subtract)):
                        dve.tensor_tensor(t2[:, c % 2, 2 * n:2 * n + 2, :], t1[:, c % 2, 0:2, :], t1[:, c % 2, 2:4, :], op).then_inc(s_t2, 1)
                if c < STAGES:
                    butterfly(c)
                if c >= 1:
                    for k in range(KH):
                        dve.wait_ge(s_hi, KH * (c - 1) + k + 1)
                        dve.scalar_tensor_tensor(wo[:, (c - 1) % 2, 1, k, :], banks[4 * ((c - 1) % 2) + k][:],
                                                 s["sug"][:, k:k + 1], wo[:, (c - 1) % 2, 0, k, :].bitcast(F32),
                                                 ALU.mult, ALU.subtract).then_inc(s_lo, 1)
            for i in range(NP):
                piece = NC + i
                dve.wait_ge(s_chi, 4 * (i + 1))
                for k in range(4):
                    scale = pr[:, P_NW + 4 * (i - 5) + k:P_NW + 4 * (i - 5) + k + 1] if i >= 5 else 1.0
                    ins = dve.scalar_tensor_tensor(wo[:, piece % 2, 1, k, :], raw[:, piece % 2, k, :], scale,
                                                   wo[:, piece % 2, 0, k, :].bitcast(F32), ALU.mult, ALU.subtract)
                ins.then_inc(s_clo, 1)
            for j in range(FB + 1):
                if j < FB:
                    dve.wait_ge(s_dm, j + 1)
                    wait(dve, s_dlo, j - 1)
                    dve.scalar_tensor_tensor(sc[:, j % 2, :], banks[j % 8][:], s["sud"][:, j:j + 1],
                                             pr[:, P_WDP:P_WDP + HID], ALU.mult, ALU.mult).then_inc(s_dsc, 1)
                if j >= 1:
                    i = j - 1
                    dve.wait_ge(s_dhi, i + 1)
                    o = wo[:, (NC + NP + i // 4) % 2, :, i % 4, :]
                    dve.tensor_tensor(o[:, 1, :], sc[:, i % 2, :], o[:, 0, :].bitcast(F32), ALU.subtract).then_inc(s_dlo, 1)


def rsqrt(eng, ch, y, v, t, scale=1.0):
    I32 = mybir.dt.int32
    ch.step(eng.tensor_scalar(v, v, scale, EPS, ALU.mult, ALU.add))
    ch.step(eng.tensor_scalar(y.bitcast(I32), v.bitcast(I32), 1, None, ALU.arith_shift_right))
    ch.done(eng.tensor_scalar(v, v, -0.5, None, ALU.mult))
    ch.sync()
    ch.step(eng.tensor_scalar(y.bitcast(I32), y.bitcast(I32), -1.0, float(0x5F3759DF), ALU.mult, ALU.add))
    for _ in range(4):
        ch.step(eng.tensor_tensor(t, y, y, ALU.mult))
        ch.step(eng.tensor_tensor(t, t, v, ALU.mult))
        ch.step(eng.scalar_tensor_tensor(y, t, 1.5, y, ALU.add, ALU.mult))


def normalize(dve, st, mv, xn, tiles, ch, free):
    for i, t in enumerate(tiles):
        ch.done(dve.bn_stats(st[:, i, :], t))
    yield
    ch.sync()
    mean, var, d, rstd = (mv[:, i, :] for i in range(4))
    ch.done(dve.tensor_tensor(mean, st[:, :, 1], st[:, :, 4], ALU.add))
    ch.done(dve.tensor_tensor(var, st[:, :, 2], st[:, :, 5], ALU.add))
    ch.step(dve.tensor_tensor(d, st[:, :, 1], st[:, :, 4], ALU.subtract))
    ch.done(dve.tensor_scalar(mean, mean, 0.5, None, ALU.mult))
    ch.step(dve.scalar_tensor_tensor(d, d, 0.25, d, ALU.mult, ALU.mult))
    ch.step(dve.scalar_tensor_tensor(var, var, 1.0 / HID, d, ALU.mult, ALU.add))
    rsqrt(dve, ch, rstd, var, d)
    yield
    for i, t in enumerate(tiles):
        sem = free(i)
        dve.tensor_scalar(xn[:, i, :], t, mean[:, i:i + 1], rstd[:, i:i + 1], ALU.subtract, ALU.mult).then_inc(sem, 1)


def ffn(nc, s, tag, ug_s, dn_s, wsc):
    res, cs, banks = s["res"], s["cs"], s["banks"]
    with ExitStack() as ctx:
        def sb(name, shape, dt=F32):
            return ctx.enter_context(nc.sbuf_tensor(f"f{tag}_{name}", shape, dt))

        def sem(name):
            return ctx.enter_context(nc.semaphore(f"f{tag}_{name}"))

        xT = sb("xT", [P, 2, KH, TOK], F32R)
        xn = sb("xn", [P, TPG, HID])
        st, mv = sb("st", [P, TPG, 6]), sb("mv", [P, 4, TPG])
        wu = [sb(f"wu{i}", [P, 2, KH, 2 * CH], F32R) for i in range(2)]
        wd = [sb(f"wd{i}", [P, 2, 2, HID], F32R) for i in range(2)]
        sc = [sb(f"sc{i}", [P, 4], F32) for i in range(2)]
        sil = sb("sil", [P, 2, 512])
        hf = sb("hf", [P, 2, 512])
        hb = sb("hb", [P, 2, 2, 2, 512], F32R)
        s_wu = [sem("wu0s"), sem("wu1s")]
        s_wd = [sem("wd0s"), sem("wd1s")]
        s_u, s_sil, s_h, s_hi, s_lo, s_d, s_acc = (sem(n) for n in ("u", "sils", "h", "hi", "lo", "d", "acc"))
        s_own, s_xn, s_tr, s_xhi, s_xlo = (sem(n) for n in ("own", "xns", "tr", "xhi", "xlo"))
        U, D, T = banks[0:4], banks[4:6], banks[6:8]
        block = ctx.enter_context(nc.Block())

        @block.sync
        def _(sp):
            def load(c, p):
                wait(sp, s_d, 16 * (c - 1))
                wait(sp, s_wu[p], 0 if isinstance(c, int) else 32)
                for dst, src, landed in ((wu[p][:].rearrange("p h k n -> p (h k n)").bitcast(F32), ug_s, s_wu),
                                         (sc[p][:], wsc, s_wu),
                                         (wd[p][:].rearrange("p h k n -> p (h k n)").bitcast(F32), dn_s, s_wd)):
                    sp.dma_start(dst, src[bass.ds(c, 1)].rearrange("c p n -> (c p) n")).then_inc(landed[p], 16)
            load(0, 0)
            load(1, 1)
            with sp.Fori(1, NC // 2) as c2:
                load(2 * c2, 0)
                load(2 * c2 + 1, 1)

        @block.tensor
        def _(pe):
            def turn(g):
                for i in range(TPG):
                    t = TPG * g + i
                    pe.wait_ge(s_xn, t + 1)
                    wait(pe, s_xlo, t - 1)
                    for k in range(KH):
                        ins = pe.transpose(T[i % 2][:, k * P:(k + 1) * P], xn[:, i, k * P:(k + 1) * P], cs[:, C_I4:C_I4 + P])
                    ins.then_inc(s_tr, 1)

            def up(n, c2, m):
                g, p = m % 4, m // 4
                if isinstance(n, int) and n < 4:
                    pe.wait_ge(s_xlo, TPG * (g + 1))
                if g == 0:
                    pe.wait_ge(s_wu[p], 32 * c2 + 32)
                for j in range(4):
                    wait(pe, s_sil if j < 2 else s_h, 2 * n - 1 + j % 2)
                    for k in range(KH):
                        for a, b in PASSES:
                            ins = pe.matmul(U[j][:], wu[p][:, a, k, j * P:(j + 1) * P], xT[:, b, k, g * 512:(g + 1) * 512],
                                            start=(k == 0 and (a, b) == PASSES[0]), stop=(k == KH - 1 and (a, b) == PASSES[-1]))
                    ins.then_inc(s_u, 1)

            def down(n, c2, m):
                g, p = m % 4, m // 4
                if g == 0:
                    pe.wait_ge(s_wd[p], 16 * c2 + 16)
                pe.wait_ge(s_lo, 2 * n + 2)
                for t in range(TPG):
                    wait(pe, s_acc, 4 * n + t - 1)
                    for j in range(2):
                        for a, b in PASSES:
                            ins = pe.matmul(D[t % 2][:], hb[:, m % 2, a, j, t * P:(t + 1) * P], wd[p][:, b, j, :],
                                            start=(j == 0 and (a, b) == PASSES[0]), stop=(j == 1 and (a, b) == PASSES[-1]))
                    ins.then_inc(s_d, 1)

            def body(c2):
                first = isinstance(c2, int)
                for m in range(8):
                    n = 8 * c2 + m
                    up(n, c2, m)
                    if first and m < 3:
                        turn(m + 1)
                    if m:
                        down(n - 1, c2, m - 1)
                    elif not first:
                        down(n - 1, c2 - 1, 7)
            turn(0)
            body(0)
            with pe.Fori(1, NC // 2) as c2:
                body(c2)
            down(4 * NC - 1, NC // 2 - 1, 7)

        @block.scalar
        def _(act):
            def turn(g):
                for i in range(TPG):
                    t = TPG * g + i
                    act.wait_ge(s_tr, t + 1)
                    act.copy(xT[:, 0, :, t * P:(t + 1) * P], T[i % 2][:].rearrange("p (k n) -> p k n", k=KH)).then_inc(s_xhi, 1)

            def body(c2):
                first = isinstance(c2, int)
                for m in range(8):
                    n, p = 8 * c2 + m, m // 4
                    if m % 4 == 0:
                        act.wait_ge(s_wu[p], 32 * c2 + 32)
                    for j in range(2):
                        act.wait_ge(s_u, 4 * n + j + 1)
                        wait(act, s_h, 2 * n - 1 + j)
                        act.activation(sil[:, j, :], U[j][:], ACT.Silu, scale=sc[p][:, j:j + 1]).then_inc(s_sil, 1)
                    for j in range(2):
                        act.wait_ge(s_h, 2 * n + j + 1)
                        wait(act, s_d, 4 * n - 4)
                        act.copy(hb[:, m % 2, 0, j, :], hf[:, j, :]).then_inc(s_hi, 1)
                    if first and m < 3:
                        turn(m + 1)
            turn(0)
            body(0)
            with act.Fori(1, NC // 2) as c2:
                body(c2)

        @block.vector
        def _(dve):
            own = Chain(dve, s_own)

            def rows(g):
                def free(i):
                    wait(dve, s_tr, TPG * (g - 1) + i + 1)
                    return s_xn
                wait(dve, s_xn, TPG * g)
                run(normalize(dve, st, mv, xn, [res[:, TPG * g + i, :] for i in range(TPG)], own, free))

            def turn(g):
                for i in range(TPG):
                    t = TPG * g + i
                    dve.wait_ge(s_xhi, t + 1)
                    at = slice(t * P, (t + 1) * P)
                    dve.tensor_tensor(xT[:, 1, :, at], T[i % 2][:].rearrange("p (k n) -> p k n", k=KH),
                                      xT[:, 0, :, at].bitcast(F32), ALU.subtract).then_inc(s_xlo, 1)

            def add(n, m):
                for t in range(TPG):
                    dve.wait_ge(s_d, 4 * n + t + 1)
                    r = res[:, TPG * (m % 4) + t, :]
                    dve.tensor_tensor(r, D[t % 2][:], r, ALU.add).then_inc(s_acc, 1)

            def body(c2):
                first = isinstance(c2, int)
                for m in range(8):
                    n, p = 8 * c2 + m, m // 4
                    if first and m < 3:
                        rows(m + 1)
                    if m % 4 == 0:
                        dve.wait_ge(s_wu[p], 32 * c2 + 32)
                    for j in range(2):
                        dve.wait_ge(s_sil, 2 * n + j + 1)
                        dve.wait_ge(s_u, 4 * n + j + 3)
                        wait(dve, s_hi, 2 * n - 1 + j)
                        wait(dve, s_lo, 2 * n - 1 + j)
                        dve.scalar_tensor_tensor(hf[:, j, :], U[2 + j][:], sc[p][:, 2 + j:3 + j], sil[:, j, :],
                                                 ALU.mult, ALU.mult).then_inc(s_h, 1)
                    for j in range(2):
                        dve.wait_ge(s_hi, 2 * n + j + 1)
                        dve.tensor_tensor(hb[:, m % 2, 1, j, :], hf[:, j, :], hb[:, m % 2, 0, j, :].bitcast(F32),
                                          ALU.subtract).then_inc(s_lo, 1)
                    if first and m < 3:
                        turn(m + 1)
                    if not (first and m == 0):
                        add(n - 1, (m - 1) % 8)
            rows(0)
            turn(0)
            body(0)
            with dve.Fori(1, NC // 2) as c2:
                body(c2)
            add(4 * NC - 1, 7)


def mixer(nc, s, in_s, out_s):
    res, cs, pr, banks, i2r, ones = s["res"], s["cs"], s["pr"], s["banks"], s["i2r"], s["ones"]
    RING = 4
    LCONV = 2 + NB
    POOL_M = {0: (2, 3), 1: (2, 3)}
    MIX = (5, 9, 12, 14, 15, 17, 19, 21, 25)
    FIRST = 5
    USES = ([("in", 0, n) for n in range(FIRST, NIN)] + [("in", 1, n) for n in range(FIRST)]
            + [("out", 0, b) for b in range(NB)])
    LEAD = [u for u in USES if u[1]]
    LAST = [u for u in USES if not u[1]]
    with ExitStack() as ctx:
        def sb(name, shape, dt=F32):
            return ctx.enter_context(nc.sbuf_tensor(f"m_{name}", shape, dt))

        def sem(name):
            return ctx.enter_context(nc.semaphore(f"ms_{name}"))

        xn, st, mv = sb("xn", [P, TPG, HID]), sb("st", [P, TPG, 6]), sb("mv", [P, 4, TPG])
        xT = sb("xT", [P, 2, KH, SEQ], F32R)
        ring = [sb(f"w{i}", [P, 2, HID], F32R) for i in range(RING)]
        xr = sb("xr", [P, 2, SEQ + 4])
        cv = sb("cv", [P, 2, SEQ])
        xc, zs = sb("xc", [P, 2, SEQ]), sb("zs", [P, 2, SEQ])
        Bf, Cf = sb("Bf", [P, SEQ]), sb("Cf", [P, SEQ])
        du, de, dw, dl, dtf = (sb(n, [P, SEQ]) for n in ("du", "de", "dw", "dl", "dtf"))
        da = sb("da", [P, SEQ])
        ec = sb("ec", [P, SEQ])
        aS, eS = sb("aS", [P, SEQ], F32R), sb("eS", [P, SEQ], F32R)
        dg = sb("dg", [HEADS, 2, HEADS])
        GT = sb("GT", [P, SEQ])
        Bt = sb("Bt", [P, 3, STATE])
        dd = sb("dd", [P, 6 * HEADS])
        xp = sb("xp", [P, 2, NCK, HPB, 32])
        L = sb("L", [P, 2, 4, SEQ])
        xd = sb("xd", [P, 2, 3, P])
        sta = sb("sta", [P, 2, 3, P])
        ex, z, y = sb("ex", [P, 2, SEQ]), sb("z", [P, 2, SEQ]), sb("y", [P, 2, SEQ])
        yh = sb("yh", [P, NB, 2, SEQ], F32R)
        sq, ss = sb("sq", [P, SEQ]), sb("ss", [P, SEQ])
        rr = sb("rr", [P, 3 * TPG])
        i2x = sb("i2x", [P, INTER], F32R)
        (s_xn, s_tr, s_xhi, s_xlo, s_in, s_os, s_pev, s_raw, s_cv, s_xcv, s_zs, s_u, s_e, s_ln, s_a, s_ah, s_eh,
         s_nu, s_dw, s_dt, s_as, s_ec, s_es, s_dg, s_G, s_B, s_D, s_gt, s_bt, s_dd, s_X, s_xp, s_A, s_sc,
         s_xd, s_mv, s_mp, s_Y, s_S, s_st, s_O, s_E, s_ex, s_y, s_z, s_yf, s_ss, s_yh, s_yl, s_V, s_v,
         s_op, s_fin, s_own, s_po, s_z0) = (sem(n) for n in (
             "xn tr xhi xlo in os pev raw cv xcv zs u e ln a ah eh nu dw dt as ec es dg G B D gt bt dd X xp A sc "
             "xd mv mp Y S st O E ex y z yf ss yh yl V v op fin own po z0").split())
        s_w = [sem(f"w{i}") for i in range(RING)]
        PB, A, Y, X, S, O = banks[0:2], banks[2:4], banks[4], banks[5], banks[6], banks[7]
        OUT = [PB[0], PB[1], S, Y]
        I = cs[:, C_I4:C_I4 + P]
        order = [BI_DT, BI_B, BI_C] + [i for b in range(NB) for i in (NB + b, b)]

        def ck(c):
            return slice(c * P, (c + 1) * P)

        def slot(use):
            return USES.index(use) % RING

        def loaded(q, use, uses):
            count = lambda some: sum(slot(u) == slot(use) for u in some)
            return 16 * (count(LEAD) + count(USES) * q + count(uses[:uses.index(use)]) + 1)

        def used(q, use):
            what, on, n = use
            if what == "in":
                return s_in, NIN * (q + on) + n + 1
            if n < NB - 1:
                return s_os, (NB - 1) * q + n + 1
            return s_op, TPG * (q + 1)

        block = ctx.enter_context(nc.Block())

        def over_sequences(eng, ahead, body):
            ahead(0)
            body(0, USES)
            with eng.Fori(1, BATCH - 1) as q:
                body(q, USES)
            body(BATCH - 1, LAST)

        @block.sync
        def _(sp):
            def load(use):
                what, _, n = use
                src = in_s[order[n]] if what == "in" else out_s[n]
                sp.dma_start(ring[slot(use)][:].rearrange("p h n -> p (h n)").bitcast(F32), src).then_inc(s_w[slot(use)], 16)

            def ahead(q):
                for i, use in enumerate(LEAD):
                    if i >= RING:
                        wait(sp, *used(-1, LEAD[i - RING]))
                    load(use)

            def body(q, uses):
                first = isinstance(q, int) and q == 0
                for use in uses:
                    before = [(q, u) for u in uses[:uses.index(use)] if slot(u) == slot(use)]
                    before = before or [(q - 1, u) for u in USES if slot(u) == slot(use) and (u in LEAD or not first)]
                    if before:
                        wait(sp, *used(*before[-1]))
                    load(use)
            over_sequences(sp, ahead, body)

        @block.tensor
        def _(pe):
            def in_proj(q, n, value):
                at = slot(("in", int(n < FIRST), n))
                w = ring[at][:].rearrange("p h (k m) -> p h k m", k=KH)
                for k in range(KH):
                    for i, (a, b) in enumerate(PASSES):
                        if k == 0 and i == 0:
                            pe.wait_ge(s_w[at], value)
                            pe.wait_ge(s_xlo, TPG * (q + 1))
                            wait(pe, s_pev, NIN * q + n - 1 if n >= 2 else NIN * q)
                        ins = pe.matmul(PB[n % 2][:], w[:, a, k, :], xT[:, b, k, :],
                                        start=(k == 0 and i == 0), stop=(k == KH - 1 and i == 2))
                        if k == KH - 1 and i == 2:
                            ins.then_inc(s_in, 1)
                        yield

            def turn(q):
                for i in range(TPG):
                    pe.wait_ge(s_xn, TPG * q + i + 1)
                    wait(pe, s_xlo, TPG * q + i - 1)
                    wait(pe, s_pev, NIN * q)
                    for k in range(KH):
                        ins = pe.transpose(PB[i % 2][:, ck(k)], xn[:, i, ck(k)], I)
                    ins.then_inc(s_tr, 1)

            def prepare_heads(q):
                pe.wait_ge(s_xcv, LCONV * q + 2)
                wait(pe, s_z, NB * q)
                for c in range(NCK):
                    ins = pe.matmul(O[:, ck(c)], Bf[:, ck(c)], Cf[:, ck(c)], start=True, stop=True)
                ins.then_inc(s_G, 1)
                yield
                pe.wait_ge(s_gt, q + 1)
                for c in range(3):
                    ins = pe.transpose(O[:, ck(c)], Bf[:, ck(c)], I)
                ins.then_inc(s_B, 1)
                yield
                pe.wait_ge(s_dt, q + 1)
                wait(pe, s_ex, NB * q)
                pe.wait_ge(s_dg, q + 1)
                for i in range(2):
                    pe.matmul(X[:, HEADS * (4 + i):HEADS * (5 + i)], ones[0:HEADS, :], dg[:, i, :], start=True, stop=True)
                for c in range(NCK):
                    ins = pe.transpose(X[:, HEADS * c:HEADS * (c + 1)], dtf[0:HEADS, ck(c)], cs[0:HEADS, C_I4:C_I4 + HEADS])
                ins.then_inc(s_D, 1)

            def decays(q, n):
                if n == 0:
                    pe.wait_ge(s_as, q + 1)
                wait(pe, s_sc, 64 * q + n - 1)
                h = n // 8 * HPB + 2 * (n % 4) + n // 4 % 2
                pe.matmul(A[n % 2][:], i2r[:, h:h + 1].to_broadcast([P, P]), aS[:], start=True, stop=True).then_inc(s_A, 1)

            def x_rows(q, b):
                pe.wait_ge(s_xcv, LCONV * q + 2 + b + 1)
                if b == 0:
                    pe.wait_ge(s_dd, q + 1)
                elif b == 1:
                    pe.wait_ge(s_xp, NB * q + 1)
                else:
                    pe.wait_ge(s_ex, NB * q + b - 1)
                for c in range(NCK):
                    ins = pe.transpose(X[:, ck(c)], xc[:, b % 2, ck(c)], I)
                ins.then_inc(s_X, 1)

            def head(q):
                yield from prepare_heads(q)
                yield
                x_rows(q, 0)
                for n in range(6):
                    decays(q, n)
                    yield

            def ahead(q):
                turn(q)
                for use in LEAD:
                    run(in_proj(q, use[2], loaded(q - 1, use, USES) if not isinstance(q, int) or q else
                                16 * (sum(slot(u) == slot(use) for u in LEAD[:LEAD.index(use)]) + 1)))
                run(head(q))

            def body(q, uses):
                def ydiag(qd):
                    b, e = qd // 2, qd % 2
                    if e == 0:
                        wait(pe, s_y, NB * q + b)
                    pe.wait_ge(s_xp, NB * q + b + 1)
                    pe.wait_ge(s_mv, 2 * NB * q + qd + 1)
                    pe.wait_ge(s_mp, 2 * NB * q + qd + 1)
                    for c in range(NCK):
                        for j in range(4):
                            ins = pe.matmul(Y[32 * j:32 * j + 32, ck(c)], xp[:, b % 2, c, 2 * j + e, :], L[:, e, j, ck(c)],
                                            start=(e == 0 and c == 0), stop=(e == 1), skip_group_check=True)
                    ins.then_inc(s_Y, 1)

                def new_states(b):
                    pe.wait_ge(s_xd, 2 * (NB * q + b + 1))
                    if b:
                        pe.wait_ge(s_st, NB * q + b)
                    else:
                        pe.wait_ge(s_bt, q + 1)
                    for c in range(3):
                        ins = pe.matmul(S[:, ck(c)], Bt[:, c, :], xd[:, b % 2, c, :], start=True, stop=True)
                    ins.then_inc(s_S, 1)

                def tail(b):
                    ydiag(2 * b + 1)
                    if b < NB - 1:
                        pe.wait_ge(s_xp, NB * q + b + 2)
                    else:
                        pe.wait_ge(s_ex, NB * q + b)
                    if b == 0:
                        pe.wait_ge(s_es, q + 1)
                    pe.matmul(X[:], i2x[:, ck(b)], eS[:], start=True, stop=True).then_inc(s_E, 1)
                    pe.wait_ge(s_st, NB * q + b + 1)
                    wait(pe, s_z, NB * q + b)
                    if b == 0:
                        wait(pe, s_v, q)
                    for c in range(1, NCK):
                        ins = pe.matmul(O[:, ck(c)], sta[:, b % 2, c - 1, :], Cf[:, ck(c)], start=True, stop=True)
                    ins.then_inc(s_O, 1)

                def fills(i):
                    ins = [u for u in uses if u[0] == "in"]
                    if i >= len(ins):
                        return iter(())
                    return in_proj(q + ins[i][1], ins[i][2], loaded(q, ins[i], uses))

                more = uses is USES
                for b in range(NB):
                    if b:
                        x_rows(q, b)
                    else:
                        wait(pe, s_fin, TPG * q)
                    if b == NB - 1 and more:
                        turn(q + 1)
                    for e in range(2):
                        fill = fills(2 * b + e)
                        n = 8 * b + 4 * e
                        if e == 0 and b:
                            new_states(b - 1)
                        for j in range(2, 6):
                            if n == 0:
                                due = 2 + j if j >= 4 else None
                            else:
                                due = n + j if 8 <= n + j < 8 * NB else None
                            if due:
                                decays(q, due)
                            for _ in range(2):
                                next(fill, None)
                        run(fill)
                        if e == 1:
                            ydiag(2 * b)
                        elif b:
                            tail(b - 1)
                run(fills(2 * NB))
                new_states(NB - 1)
                tail(NB - 1)
                run(fills(2 * NB + 1))
                run(fills(2 * NB + 2))
                pe.wait_ge(s_pev, NIN * q + NIN + (FIRST if more else 0))
                pe.wait_ge(s_st, NB * (q + 1))
                pe.wait_ge(s_y, NB * (q + 1))
                following = head(q + 1) if more else iter(())
                for b in range(NB):
                    at = slot(("out", 0, b))
                    pe.wait_ge(s_w[at], loaded(q, ("out", 0, b), uses))
                    pe.wait_ge(s_yl, NB * q + b + 1)
                    if b == NB - 2:
                        pe.wait_ge(s_ss, NB * (q + 1))
                        pe.wait_ge(s_z, NB * (q + 1))
                        if more:
                            pe.wait_ge(s_bt, q + 2)
                        for t in range(TPG):
                            ins = pe.matmul(O[:, t:t + 1], ss[:, ck(t)], ones[:, 0:1], start=True, stop=True)
                        ins.then_inc(s_V, 1)
                    for t in range(TPG):
                        for i, (m, n) in enumerate(PASSES):
                            ins = pe.matmul(OUT[t][:], yh[:, b, m, ck(t)], ring[at][:, n, :],
                                            start=(b == 0 and i == 0), stop=(b == NB - 1 and i == 2))
                        if b == NB - 1:
                            ins.then_inc(s_op, 1)
                        elif t == TPG - 1:
                            ins.then_inc(s_os, 1)
                        if TPG * b + t in MIX:
                            next(following, None)
                run(following)
            over_sequences(pe, ahead, body)

        @block.scalar
        def _(act):
            def raw(q, n, col):
                at = (1, 2)[n] if n < 2 else 3 + 2 * (n - 2)
                act.wait_ge(s_in, NIN * q + at + 1)
                wait(act, s_cv, LCONV * q + n - 1)
                wait(act, s_xcv, LCONV * q + n - 1)
                act.copy(xr[:, n % 2, 3:3 + SEQ], PB[at % 2][:])
                w = P_CW + 4 * col
                act.activation(cv[:, n % 2, :], PB[at % 2][:], ACT.Identity, scale=pr[:, w + 3:w + 4],
                               bias=pr[:, P_CB + col:P_CB + col + 1]).then_inc(s_pev, 1)

            def conv_silu(q, n, dst):
                act.wait_ge(s_cv, LCONV * q + n + 1)
                act.activation(dst, cv[:, n % 2, :], ACT.Silu).then_inc(s_xcv, 1)

            def x_silu(q, b):
                wait(act, s_X, NB * q + b - 1)
                wait(act, s_y, NB * q + b - 1)
                conv_silu(q, 2 + b, xc[:, b % 2, :])

            def gate(q, b):
                act.wait_ge(s_in, NIN * q + 5 + 2 * b)
                wait(act, s_yf, NB * q + b - 1)
                act.activation(zs[:, b % 2, :], PB[(4 + 2 * b) % 2][:], ACT.Silu).then_inc(s_pev, 1)

            def turn(q):
                for i in range(TPG):
                    act.wait_ge(s_tr, TPG * q + i + 1)
                    wait(act, s_in, NIN * q)
                    act.copy(xT[:, 0, :, ck(i)], PB[i % 2][:].rearrange("p (k n) -> p k n", k=KH)).then_inc(s_xhi, 1)

            def times(q, b):
                act.wait_ge(s_E, NB * q + b + 1)
                wait(act, s_z, NB * q + b - 1)
                act.copy(ex[:, b % 2, :], X[:]).then_inc(s_ex, 1)

            def high(q, b):
                act.wait_ge(s_yf, NB * q + b + 1)
                wait(act, s_op, TPG * q)
                act.copy(yh[:, b, 0, :], y[:, b % 2, :]).then_inc(s_yh, 1)

            def first(q, between):
                act.wait_ge(s_in, NIN * q + 1)
                wait(act, s_dt, q)
                act.activation(du[:], PB[0][:], ACT.Identity, bias=pr[:, P_DTB:P_DTB + 1]).then_inc(s_pev, 1)
                raw(q, 0, NB)
                act.wait_ge(s_nu, q + 1)
                act.activation(de[:], de[:], ACT.Exp).then_inc(s_e, 1)
                raw(q, 1, NB + 1)
                next(between, None)
                act.wait_ge(s_dw, q + 1)
                act.activation(dl[:], dw[:], ACT.Ln).then_inc(s_ln, 1)
                wait(act, s_O, NB * q)
                conv_silu(q, 0, Bf[:])
                raw(q, 2, 0)
                conv_silu(q, 1, Cf[:])
                gate(q, 0)
                act.wait_ge(s_dt, q + 1)
                wait(act, s_as, q)
                act.activation(da[:], dtf[:], ACT.Exp, scale=s["acol"][:, 0:1]).then_inc(s_a, 1)
                act.wait_ge(s_a, q + 1)
                wait(act, s_A, 64 * q)
                act.copy(aS[:], da[:]).then_inc(s_ah, 1)
                x_silu(q, 0)
                act.wait_ge(s_G, q + 1)
                wait(act, s_mp, 2 * NB * q)
                wait(act, s_mv, 2 * NB * q)
                act.copy(GT[:], O[:]).then_inc(s_gt, 1)
                act.wait_ge(s_ec, q + 1)
                wait(act, s_E, NB * q)
                act.copy(eS[:], ec[:]).then_inc(s_eh, 1)
                act.wait_ge(s_B, q + 1)
                act.copy(Bt[:].rearrange("p c n -> p (c n)"), O[:, 0:3 * P]).then_inc(s_bt, 1)

            def ahead(q):
                turn(q)
                first(q, iter(()))

            def body(q, uses):
                more = uses is USES

                def ending():
                    high(q, NB - 2)
                    times(q, NB - 1)
                    yield
                    high(q, NB - 1)
                    yield

                for b in range(NB):
                    if b < NB - 1:
                        raw(q, 3 + b, b + 1)
                    elif more:
                        turn(q + 1)
                    if b >= 2:
                        high(q, b - 2)
                    if b:
                        times(q, b - 1)
                    if b < NB - 1:
                        x_silu(q, b + 1)
                        gate(q, b + 1)
                end = ending()
                if more:
                    first(q + 1, end)
                run(end)
            over_sequences(act, ahead, body)

        @block.vector
        def _(dve):
            dve.memset(xp[:], 0.0).then_inc(s_z0, 1)
            dve.memset(xr[:, :, 0:3], 0.0).then_inc(s_z0, 1)
            dve.tensor_copy(i2x[:].rearrange("p (h d) -> p h d", d=HDIM),
                            cs[:, C_I2:C_I2 + HEADS].unsqueeze(2).to_broadcast([P, HEADS, HDIM])).then_inc(s_z0, 1)
            dve.wait_ge(s_z0, 3)
            counts = {}

            def tiles(q):
                return [res[:, bass.ds(TPG * q + i, 1), :].rearrange("p o n -> p (o n)") for i in range(TPG)]

            def rows(q, own):
                def free(i):
                    wait(dve, s_tr, TPG * (q - 1) + i + 1)
                    return s_xn
                return normalize(dve, st, mv, xn, tiles(q), own, free)

            def turn(q):
                for i in range(TPG):
                    dve.wait_ge(s_xhi, TPG * q + i + 1)
                    dve.tensor_tensor(xT[:, 1, :, ck(i)], PB[i % 2][:].rearrange("p (k n) -> p k n", k=KH),
                                      xT[:, 0, :, ck(i)].bitcast(F32), ALU.subtract).then_inc(s_xlo, 1)

            def conv(q, n, col, own):
                dve.wait_ge(s_pev, NIN * q + ((1, 2)[n] if n < 2 else 3 + 2 * (n - 2)) + 1)
                w = P_CW + 4 * col
                for k in range(3):
                    ins = dve.scalar_tensor_tensor(cv[:, n % 2, :], xr[:, n % 2, k:k + SEQ], pr[:, w + k:w + k + 1],
                                                   cv[:, n % 2, :], ALU.mult, ALU.add)
                    if k < 2:
                        own.step(ins)
                ins.then_inc(s_cv, 1)

            def quad_scans(q, qd):
                for j in range(4):
                    n = 4 * qd + j
                    dve.wait_ge(s_A, 64 * q + n + 1)
                    wait(dve, s_Y, 2 * NB * q + qd - 1)
                    dve.tensor_tensor_scan(L[:, qd % 2, j, :], A[n % 2][:], cs[:, C_I4:C_I4 + SEQ], 0.0,
                                           ALU.mult, ALU.add).then_inc(s_sc, 1)

            def padded(q, b):
                dve.wait_ge(s_X, NB * q + b + 1)
                wait(dve, s_Y, 2 * (NB * q + b - 1))
                xv = X[:].rearrange("p (c j e d) -> p c j e d", c=NCK, j=4, e=2)
                dv = dd[:, 0:NCK * HEADS].rearrange("p (c h) -> p c h", c=NCK)
                pv = xp[:, b % 2].rearrange("p c (j e) m -> p c j e m", e=2)
                for e in range(2):
                    dt = dv[:, :, HPB * b + e:HPB * (b + 1):2].unsqueeze(3).to_broadcast([P, NCK, 4, HDIM])
                    ins = dve.tensor_tensor(pv[:, :, :, e, HDIM * e:HDIM * (e + 1)], xv[:, :, :, e, :], dt, ALU.mult)
                ins.then_inc(s_xp, 1)

            def decayed(q, qd):
                b, e = qd // 2, qd % 2
                dve.wait_ge(s_sc, 64 * q + 4 * qd + 4)
                dve.wait_ge(s_xp, NB * q + b + 1)
                wait(dve, s_S, NB * q + b - 1)
                pv = xp[:, b % 2].rearrange("p c (j e) m -> p c j e m", e=2)[:, 0:3, :, e, HDIM * e:HDIM * (e + 1)]
                last = L[:, e].rearrange("p j (c l) -> p c j l", c=NCK)[:, 0:3, :, P - 1:P].to_broadcast([P, 3, 4, HDIM])
                out = xd[:, b % 2].rearrange("p c (j e d) -> p c j e d", j=4, e=2)[:, :, :, e, :]
                dve.tensor_tensor(out, pv, last, ALU.mult).then_inc(s_xd, 1)

            def times_g(q, qd):
                e = qd % 2
                dve.wait_ge(s_xd, 2 * NB * q + qd + 1)
                for j in range(4):
                    if j not in POOL_M[e]:
                        ins = dve.tensor_tensor(L[:, e, j, :], L[:, e, j, :], GT[:], ALU.mult)
                ins.then_inc(s_mv, 1)

            def even_heads(q, b):
                quad_scans(q, 2 * b)
                padded(q, b)
                decayed(q, 2 * b)
                times_g(q, 2 * b)

            def first(q, own, between):
                dve.wait_ge(s_pev, NIN * q + 1)
                wait(dve, s_es, q)
                dve.scalar_tensor_tensor(de[:], du[:], -1.0, du[:], ALU.mult, ALU.min).then_inc(s_nu, 1)
                conv(q, 0, NB, own)
                next(between, None)
                dve.wait_ge(s_e, q + 1)
                dve.tensor_scalar(dw[:], de[:], 1.0, None, ALU.add).then_inc(s_dw, 1)
                conv(q, 1, NB + 1, own)
                dve.wait_ge(s_dw, q + 1)
                own.step(dve.scalar_tensor_tensor(de[:], dw[:], -1.0, de[:], ALU.add, ALU.subtract))
                wait(dve, s_D, q)
                own.step(dve.reciprocal(dtf[:], dw[:]))
                own.step(dve.tensor_tensor(de[:], de[:], dtf[:], ALU.mult))
                dve.wait_ge(s_ln, q + 1)
                own.step(dve.tensor_tensor(dl[:], dl[:], de[:], ALU.subtract))
                own.step(dve.scalar_tensor_tensor(dl[:], du[:], 0.0, dl[:], ALU.max, ALU.add))
                dve.tensor_scalar(dtf[:], dl[:], 100.0, 0.0, ALU.min, ALU.max).then_inc(s_dt, 1)
                next(between, None)
                dve.wait_ge(s_a, q + 1)
                wait(dve, s_eh, q)
                for c in range(NCK):
                    ins = dve.tensor_tensor_scan(ec[:, ck(c)], da[:, ck(c)], ones[:], 1.0, ALU.mult, ALU.mult)
                ins.then_inc(s_ec, 1)
                dve.wait_ge(s_ah, q + 1)
                own.step(dve.tensor_tensor(aS[HEADS:P, :], da[HEADS:P, :], aS[HEADS:P, :].bitcast(F32), ALU.subtract))
                dve.memset(aS[:, 0:SEQ:P].bitcast(F32), 0.0).then_inc(s_as, 1)
                dve.wait_ge(s_ec, q + 1)
                for i in range(2):
                    at = (i + 2) * P - 1
                    ins = dve.tensor_scalar(dg[:, i, :], cs[0:HEADS, C_I2:C_I2 + HEADS], ec[0:HEADS, at:at + 1], None, ALU.mult)
                ins.then_inc(s_dg, 1)
                conv(q, 2, 0, own)
                next(between, None)
                dve.wait_ge(s_eh, q + 1)
                dve.tensor_tensor(eS[HEADS:P, :], ec[HEADS:P, :], eS[HEADS:P, :].bitcast(F32), ALU.subtract).then_inc(s_es, 1)
                dve.wait_ge(s_D, q + 1)
                wait(dve, s_st, NB * q)
                dve.tensor_copy(dd[:], X[:, 0:6 * HEADS]).then_inc(s_dd, 1)
                dve.wait_ge(s_gt, q + 1)
                dve.wait_ge(s_dd, q + 1)
                even_heads(q, 0)
                run(between)
                quad_scans(q, 1)

            def ahead(q):
                own = Chain(dve, s_own)
                run(rows(q, own))
                turn(q)
                first(q, own, iter(()))
                counts["ahead"] = own.n

            def body(q, uses):
                more = uses is USES
                own = Chain(dve, s_own, counts["ahead"] + counts.get("turn", 0) * q)

                def states(b):
                    dve.wait_ge(s_S, NB * q + b + 1)
                    wait(dve, s_O, NB * q + b - 1)
                    own.step(dve.tensor_copy(sta[:, b % 2, 0, :], S[:, ck(0)]))
                    for i in range(2):
                        at = HEADS * (4 + i) + HPB * b
                        decay = dd[:, at:at + HPB].unsqueeze(2).to_broadcast([P, HPB, HDIM])
                        own.step(dve.tensor_tensor(sta[:, b % 2, i + 1, :].rearrange("p (h d) -> p h d", h=HPB),
                                                   sta[:, b % 2, i, :].rearrange("p (h d) -> p h d", h=HPB), decay, ALU.mult))
                        ins = dve.tensor_tensor(sta[:, b % 2, i + 1, :], S[:, ck(i + 1)], sta[:, b % 2, i + 1, :], ALU.add)
                        if i == 0:
                            own.step(ins)
                    ins.then_inc(s_st, 1)

                def within(b):
                    dve.wait_ge(s_Y, 2 * (NB * q + b + 1))
                    wait(dve, s_ss, NB * q + b - 1)
                    wait(dve, s_yh, NB * q + b - 1)
                    wait(dve, s_yl, NB * q + b - 1)
                    dve.scalar_tensor_tensor(y[:, b % 2, :], xc[:, b % 2, :], pr[:, P_D + b:P_D + b + 1], Y[:],
                                             ALU.mult, ALU.add).then_inc(s_y, 1)

                def carried(b):
                    wait(dve, s_yf, NB * q + b - 1)
                    dve.wait_ge(s_O, NB * q + b + 1)
                    dve.wait_ge(s_ex, NB * q + b + 1)
                    dve.tensor_tensor(z[:, b % 2, P:SEQ], O[:, P:SEQ], ex[:, b % 2, P:SEQ], ALU.mult).then_inc(s_z, 1)

                def ending():
                    states(NB - 1)
                    yield
                    within(NB - 1)
                    carried(NB - 1)
                    yield
                    yield
                    dve.wait_ge(s_V, q + 1)
                    dve.tensor_copy(rr[:, 0:TPG], O[:, 0:TPG]).then_inc(s_v, 1)
                    dve.wait_ge(s_v, q + 1)
                    rsqrt(dve, own, rr[:, TPG:2 * TPG], rr[:, 0:TPG], rr[:, 2 * TPG:3 * TPG], 1.0 / INTER)
                    for t, tile in enumerate(tiles(q)):
                        dve.wait_ge(s_op, TPG * q + t + 1)
                        dve.scalar_tensor_tensor(tile, OUT[t][:], rr[:, TPG + t:TPG + t + 1], tile,
                                                 ALU.mult, ALU.add).then_inc(s_fin, 1)
                    yield

                following = rows(q + 1, own) if more else iter(())
                for b in range(NB):
                    if b == NB - 1 and more:
                        turn(q + 1)
                    if b:
                        even_heads(q, b)
                    if b:
                        states(b - 1)
                        within(b - 1)
                    if b:
                        quad_scans(q, 2 * b + 1)
                    decayed(q, 2 * b + 1)
                    times_g(q, 2 * b + 1)
                    if b < NB - 1:
                        conv(q, 3 + b, b + 1, own)
                    if b:
                        carried(b - 1)
                    if b in (3, 4, 5):
                        next(following, None)
                end = ending()
                if more:
                    first(q + 1, own, end)
                run(end)
                counts.setdefault("turn", own.n)
            over_sequences(dve, ahead, body)

        @block.gpsimd
        def _(pool):
            def times_g(q, qd):
                e = qd % 2
                if qd == 0:
                    pool.wait_ge(s_gt, q + 1)
                pool.wait_ge(s_xd, 2 * NB * q + qd + 1)
                for j in POOL_M[e]:
                    ins = pool.tensor_tensor(L[:, e, j, :], L[:, e, j, :], GT[:], ALU.mult)
                ins.then_inc(s_mp, 1)

            def body(q, uses):
                own = Chain(pool, s_po, (2 * NB - 1) * q)

                def combine(b):
                    pool.wait_ge(s_z, NB * q + b + 1)
                    v = y[:, b % 2, :]
                    own.step(pool.tensor_tensor(y[:, b % 2, P:SEQ], y[:, b % 2, P:SEQ], z[:, b % 2, P:SEQ], ALU.add))
                    pool.wait_ge(s_pev, NIN * q + 5 + 2 * b)
                    pool.tensor_tensor(v, v, zs[:, b % 2, :], ALU.mult).then_inc(s_yf, 1)
                    pool.wait_ge(s_yf, NB * q + b + 1)
                    wait(pool, s_ss, NB * q + b)
                    if b == 0:
                        wait(pool, s_V, q)
                        pool.tensor_tensor(ss[:], v, v, ALU.mult).then_inc(s_ss, 1)
                    else:
                        own.step(pool.tensor_tensor(sq[:], v, v, ALU.mult))
                        pool.tensor_tensor(ss[:], ss[:], sq[:], ALU.add).then_inc(s_ss, 1)

                def low(b):
                    pool.wait_ge(s_yh, NB * q + b + 1)
                    pool.tensor_tensor(yh[:, b, 1, :], y[:, b % 2, :], yh[:, b, 0, :].bitcast(F32), ALU.subtract).then_inc(s_yl, 1)

                for b in range(NB):
                    if b:
                        times_g(q, 2 * b)
                    if b >= 2:
                        low(b - 2)
                    times_g(q, 2 * b + 1)
                    if b:
                        combine(b - 1)
                low(NB - 2)
                combine(NB - 1)
                low(NB - 1)
                if uses is USES:
                    times_g(q + 1, 0)
            over_sequences(pool, lambda q: times_g(q, 0), body)


def kernel(**inputs):
    import concourse.bacc as _bacc
    from concourse.bass_utils import run_bass_kernel_spmd as _run

    I = {k.split("_", 1)[1]: np.asarray(v) for k, v in inputs.items()}
    f = np.float32

    def cols(v):
        return np.ascontiguousarray(v.reshape(-1, P).T)

    def rows(wT):
        K, N = wT.shape
        return wT.reshape(K // P, P, N).transpose(1, 0, 2).reshape(P, -1)

    gate, up = I["ffn_W_gate"], I["ffn_W_up"]
    wug = np.stack([rows(np.concatenate([w[c * CH:(c + 1) * CH] for w in (gate, up)]).T) for c in range(NC)])
    sc = I["ffn_Wscale_ug"]
    wsc = np.stack([np.concatenate([cols(sc[o + c * CH:o + (c + 1) * CH]) for o in (FF, 0)], 1) for c in range(NC)])
    wdn = rows(I["ffn_W_down"].T)
    w = I["attn_in_proj_w"]
    w = np.concatenate([w, w[-HEADS:], np.zeros((P, HID), f)])
    win = np.stack([rows(w[b * P:(b + 1) * P].T) for b in range(NIN + 1)])
    wout = I["attn_out_proj_w"].T.reshape(NB, P, HID)
    had = np.ones((1, 1), f)
    while had.shape[0] < P:
        had = np.block([[had, had], [had, -had]])
    eye = np.eye(P, dtype=f)
    cst = np.concatenate([had, np.tile(eye, (1, 4)), np.tile(np.eye(HEADS, dtype=f), (2, 1))], 1)
    par = np.concatenate([
        cols(I["ffn_SU_ug"]), cols(I["ffn_SU_dp"]),
        np.tile(I["attn_A_log"], 2)[:, None], np.tile(I["attn_dt_bias"], 2)[:, None],
        cols(np.repeat(I["attn_D"], HDIM)),
        I["attn_conv_w"].reshape(10, P, 4).transpose(1, 0, 2).reshape(P, 40), cols(I["attn_conv_b"]),
        cols(I["attn_norm_w"]), np.broadcast_to(I["ffn_Wscale_dp"], (P, HID))], 1)
    arrays = dict(x=I["attn_hidden_states"].reshape(TOK, HID), wug=wug, wsc=wsc, wdn=wdn, win=win, wout=wout, cst=cst, par=par)

    nc = _bacc.Bacc("TRN2", target_bir_lowering=False, num_devices=1)
    arrays = {f"in_{k}": np.ascontiguousarray(v) for k, v in arrays.items()}
    args = [nc.dram_tensor(k, v.shape, F32, kind="ExternalInput").ap() for k, v in arrays.items()]
    args.append(nc.dram_tensor("out", (TOK, HID), F32, kind="ExternalOutput").ap())
    program(nc, *args)
    r = _run(nc, [arrays], core_ids=[0])
    return r.results[0]["out"].reshape(BATCH, SEQ, HID)
```

```python
from contextlib import ExitStack
import math

import numpy as np
import concourse.bass as bass
from concourse import mybir

F32 = mybir.dt.float32
F32R = mybir.dt.float32r
ALU = mybir.AluOpType
ACT = mybir.ActivationFunctionType

P = 128
BATCH, SEQ, HID = 4, 512, 512
TOK = BATCH * SEQ
NT = TOK // P
KH = HID // P
FF = 2048
CH = 256
NC = FF // CH
FB = FF // P
G = TOK // 512
TPG = 512 // P
INTER, STATE, HEADS, HDIM = 1024, 128, 64, 16
NB = INTER // P
HPB = P // HDIM
NIN = 2 * NB + 3
BI_B, BI_C, BI_DT = 2 * NB, 2 * NB + 1, 2 * NB + 2
NCK = SEQ // P
EPS = 1e-5

C_H, C_I4, C_I2, C_END = 0, P, P + 4 * P, P + 4 * P + HEADS
_c = np.cumsum([0, KH, FB, 1, 1, NB, 40, 10, NB, HID]).tolist()
P_SUG, P_SUD, P_ALOG, P_DTB, P_D, P_CW, P_CB, P_NW, P_WDP, P_END = _c

PASSES = ((0, 0), (0, 1), (1, 0))


def wait(eng, sem, value):
    if isinstance(value, int) and value <= 0:
        return
    eng.wait_ge(sem, value)


def run(steps):
    for _ in steps:
        pass


class Chain:

    def __init__(self, eng, sem, base=0):
        self.eng, self.sem, self.n, self.base = eng, sem, 0, base

    def done(self, ins):
        self.n += 1
        ins.then_inc(self.sem, 1)

    def sync(self):
        wait(self.eng, self.sem, self.base + self.n)

    def step(self, ins):
        self.done(ins)
        self.sync()


def program(nc, x, wug, wsc, wdn, win, wout, cst, par, out):
    ug_s = nc.dram_tensor("ug_split", [NC, P, 2 * KH * 2 * CH], F32, kind="Internal").ap()
    dn_s = nc.dram_tensor("dn_split", [NC, P, 2 * 2 * HID], F32, kind="Internal").ap()
    in_s = nc.dram_tensor("in_split", [NIN + 1, P, 2 * HID], F32, kind="Internal").ap()
    out_s = nc.dram_tensor("out_split", [NB, P, 2 * HID], F32, kind="Internal").ap()
    with ExitStack() as ctx:
        res = ctx.enter_context(nc.sbuf_tensor("res", [P, NT, HID], F32))
        cs = ctx.enter_context(nc.sbuf_tensor("cs", [P, C_END], F32))
        pr = ctx.enter_context(nc.sbuf_tensor("pr", [P, P_END], F32))
        sug = ctx.enter_context(nc.sbuf_tensor("sug", [P, KH], F32))
        sud = ctx.enter_context(nc.sbuf_tensor("sud", [P, FB], F32))
        acol = ctx.enter_context(nc.sbuf_tensor("acol", [P, 1], F32))
        i2r = ctx.enter_context(nc.sbuf_tensor("i2r", [P, HEADS], F32R))
        ones = ctx.enter_context(nc.sbuf_tensor("ones", [P, P], F32))
        xn = ctx.enter_context(nc.sbuf_tensor("xn", [P, TPG, HID], F32))
        banks = [ctx.enter_context(nc.psum_tensor(f"bank{i}", [P, 512], F32)) for i in range(8)]
        s = dict(res=res, cs=cs, pr=pr, sug=sug, sud=sud, acol=acol, i2r=i2r, ones=ones, xn=xn, banks=banks)
        prepare(nc, s, x, wug, wdn, cst, par, ug_s, dn_s)
        ffn(nc, s, "a", ug_s, dn_s, wsc, (wug, win, wout, in_s, out_s, x))
        mixer(nc, s, in_s, out_s)
        ffn(nc, s, "b", ug_s, dn_s, wsc, out=out)


def prepare(nc, s, x, wug, wdn, cst, par, ug_s, dn_s):
    res, cs, pr, banks = s["res"], s["cs"], s["pr"], s["banks"]
    with ExitStack() as ctx:
        def sb(name, shape, dt=F32):
            return ctx.enter_context(nc.sbuf_tensor(name, shape, dt))

        def sem(name):
            return ctx.enter_context(nc.semaphore(name))

        raw = sb("p_raw", [P, 2, KH, 2 * CH])
        t1 = sb("p_t1", [P, 2, KH, 2 * CH])
        wu = sb("p_wu", [P, 2, 2, KH, 2 * CH], F32R)
        da = sb("p_da", [P, FB, HID])
        db = sb("p_db", [P, FB, HID], F32R)
        wd = sb("p_wd", [P, 2, 2, 4, HID], F32R)
        s_par, s_x0, s_x, s_c, s_ex = sem("p_par"), sem("p_x0"), sem("p_x"), sem("p_c"), sem("p_ex")
        s_raw = [sem("p_raw0"), sem("p_raw1")]
        s_q = [sem(f"p_q{i}") for i in range(4)]
        s_u = [sem("p_u0"), sem("p_u1")]
        s_mm, s_hi, s_lo, s_st = sem("p_mm"), sem("p_hi"), sem("p_lo"), sem("p_st")
        s_dv, s_po, s_bd, s_bp, s_dm, s_dhi, s_dlo = (sem(f"p_{n}") for n in ("dv", "po", "bd", "bp", "dm", "dhi", "dlo"))
        s_ds = sem("p_ds")
        st, mv, s_ln = sb("p_st6", [P, TPG, 6]), sb("p_mv", [P, 4, TPG]), sem("p_ln")
        H = cs[:, C_H:C_H + P]
        QD = FB // 4
        SPLIT = 352
        block = ctx.enter_context(nc.Block())

        def down_split(q):
            return wd[:, q] if q < 2 else db[:, 8 * (q - 2):8 * (q - 1), :].rearrange("p (l b) n -> p l b n", l=2)

        def chunk_butterflies(eng, c):
            for n, op in enumerate((ALU.add, ALU.subtract)):
                eng.tensor_tensor(t1[:, c, n::2, :], raw[:, c, 0::2, :], raw[:, c, 1::2, :], op).then_inc(s_u[c], 1)
            eng.wait_ge(s_u[c], 2)
            for n, op in enumerate((ALU.add, ALU.subtract)):
                eng.tensor_tensor(raw[:, c, 2 * n:2 * n + 2, :], t1[:, c, 0:2, :], t1[:, c, 2:4, :], op).then_inc(s_u[c], 1)

        def down_stage(eng, own, cols, blocks, stage, done=None):
            w = 1 << stage
            src, dst = (v.rearrange("p (u t w) n -> p u t w n", t=2, w=w)
                        for v in (da[:, blocks, cols], db[:, blocks, cols].bitcast(F32)))
            if stage % 2:
                src, dst = dst, src
            own.sync()
            for t, op in enumerate((ALU.add, ALU.subtract)):
                at = [(slice(None), slice(None), t), (slice(None), slice(None), 0), (slice(None), slice(None), 1)]
                views = [v[i] for v, i in zip((dst, src, src), at)]
                if w == 1:
                    views = [v[:, :, 0] for v in views]
                elif src.shape[1] == 1:
                    views = [v[:, 0] for v in views]
                ins = eng.tensor_tensor(*views, op)
                if done is None:
                    own.done(ins)
                else:
                    ins.then_inc(done, 1)

        def down_quarter(eng, own, cols, q):
            eng.wait_ge(s_q[q], 16)
            blocks = slice(4 * q, 4 * q + 4)
            n = cols.stop - cols.start
            scale = pr[:, P_WDP + cols.start:P_WDP + cols.stop].unsqueeze(1).to_broadcast([P, 4, n])
            own.done(eng.tensor_tensor(da[:, blocks, cols], da[:, blocks, cols], scale, ALU.mult))
            down_stage(eng, own, cols, blocks, 0)
            down_stage(eng, own, cols, blocks, 1)

        @block.sync
        def _(sp):
            sp.dma_start(cs[:], cst).then_inc(s_par, 16)
            sp.dma_start(pr[:], par).then_inc(s_par, 16)
            sp.dma_start(raw[:, 0], wug[0].rearrange("p (k n) -> p k n", k=KH)).then_inc(s_raw[0], 16)
            for q in range(4):
                sp.dma_start(da[:, 4 * q:4 * q + 4, :],
                             wdn[:, 4 * q * HID:4 * (q + 1) * HID].rearrange("p (k n) -> p k n", k=4)).then_inc(s_q[q], 16)
                if q == 1:
                    sp.dma_start(raw[:, 1], wug[1].rearrange("p (k n) -> p k n", k=KH)).then_inc(s_raw[1], 16)
            xt = x.rearrange("(t p) n -> p t n", p=P)
            sp.dma_start(res[:, 0:TPG, :], xt[:, 0:TPG, :]).then_inc(s_x0, 16)
            sp.dma_start(res[:, TPG:2 * TPG, :], xt[:, TPG:2 * TPG, :]).then_inc(s_x, 16)
            for c in range(2):
                sp.wait_ge(s_lo, KH * (c + 1))
                sp.dma_start(ug_s[c], wu[:, c].rearrange("p h k n -> p (h k n)").bitcast(F32)).then_inc(s_st, 16)
            for q in range(QD):
                for h in range(2):
                    sp.wait_ge(s_dlo, 4 * q + 2 * (h + 1))
                    dst = dn_s[2 * q + h].rearrange("p (l j n) -> p l j n", l=2, j=2)
                    sp.dma_start(dst, down_split(q)[:, :, 2 * h:2 * h + 2, :].bitcast(F32)).then_inc(s_ds, 16)
            sp.wait_ge(s_x, 16)
            sp.wait_ge(s_st, 32)
            sp.wait_ge(s_ds, 32 * QD)

        @block.gpsimd
        def _(pool):
            own = Chain(pool, s_po)
            cols = slice(SPLIT, HID)
            pool.wait_ge(s_par, 32)
            for q in range(4):
                down_quarter(pool, own, cols, q)
                if q == 1:
                    pool.wait_ge(s_raw[1], 16)
                    chunk_butterflies(pool, 1)
            down_stage(pool, own, cols, slice(0, FB), 2)
            down_stage(pool, own, cols, slice(0, FB), 3, s_bp)

        @block.tensor
        def _(pe):
            pe.wait_ge(s_par, 32)
            for c in range(2):
                pe.wait_ge(s_u[c], 4)
                for k in range(KH):
                    pe.matmul(banks[4 * c + k][:], H, raw[:, c, k, :], start=True, stop=True).then_inc(s_mm, 1)
            for j in range(FB):
                if j % 8 == 0:
                    pe.wait_ge(s_bd, j // 8 + 1)
                    pe.wait_ge(s_bp, j // 8 + 1)
                if j < 8:
                    pe.wait_ge(s_lo, j + 1)
                else:
                    pe.wait_ge(s_dlo, j - 7)
                pe.matmul(banks[j % 8][:], H, da[:, j, :], start=True, stop=True).then_inc(s_dm, 1)

        @block.scalar
        def _(act):
            act.wait_ge(s_par, 32)
            act.activation(s["acol"][:], pr[:, P_ALOG:P_ALOG + 1], ACT.Exp).then_inc(s_ex, 1)
            act.wait_ge(s_c, 5)
            for i in range(2 * KH):
                c, k = i // KH, i % KH
                act.wait_ge(s_mm, i + 1)
                act.activation(wu[:, c, 0, k, :], banks[i][:], ACT.Copy, scale=s["sug"][:, k:k + 1]).then_inc(s_hi, 1)
            for j in range(FB):
                q = j // 4
                act.wait_ge(s_dm, j + 1)
                act.activation(down_split(q)[:, 0, j % 4, :], banks[j % 8][:], ACT.Copy, scale=s["sud"][:, j:j + 1]).then_inc(s_dhi, 1)

        @block.vector
        def _(dve):
            own = Chain(dve, s_dv)
            cols = slice(0, SPLIT)
            dve.memset(s["ones"][:], 1.0).then_inc(s_c, 1)
            dve.wait_ge(s_par, 32)
            dve.tensor_scalar(s["sug"][:], pr[:, P_SUG:P_SUG + KH], 1.0 / math.sqrt(HID), None, ALU.mult).then_inc(s_c, 1)
            dve.tensor_scalar(s["sud"][:], pr[:, P_SUD:P_SUD + FB], 0.5 / math.sqrt(FF), None, ALU.mult).then_inc(s_c, 1)
            dve.tensor_copy(s["i2r"][:], cs[:, C_I2:C_I2 + HEADS]).then_inc(s_c, 1)
            dve.wait_ge(s_ex, 1)
            dve.tensor_scalar(s["acol"][:], s["acol"][:], -1.0, None, ALU.mult).then_inc(s_c, 1)
            dve.wait_ge(s_c, 5)
            dve.wait_ge(s_raw[0], 16)
            chunk_butterflies(dve, 0)

            def chunk_low(c):
                for k in range(KH):
                    dve.wait_ge(s_hi, KH * c + k + 1)
                    dve.scalar_tensor_tensor(wu[:, c, 1, k, :], banks[4 * c + k][:], s["sug"][:, k:k + 1],
                                             wu[:, c, 0, k, :].bitcast(F32), ALU.mult, ALU.subtract).then_inc(s_lo, 1)

            for q in range(4):
                down_quarter(dve, own, cols, q)
                if q % 2 == 1:
                    chunk_low(q // 2)
            down_stage(dve, own, cols, slice(0, FB), 2)
            down_stage(dve, own, cols, slice(0, FB), 3, s_bd)
            for j in range(FB):
                q = j // 4
                dve.wait_ge(s_dhi, j + 1)
                dve.scalar_tensor_tensor(down_split(q)[:, 1, j % 4, :], banks[j % 8][:], s["sud"][:, j:j + 1],
                                         down_split(q)[:, 0, j % 4, :].bitcast(F32), ALU.mult, ALU.subtract).then_inc(s_dlo, 1)
            dve.wait_ge(s_x0, 16)
            run(normalize(dve, st, mv, s["xn"], [res[:, i, :] for i in range(TPG)], own, lambda i: s_ln))


def rsqrt(eng, ch, y, v, t, scale=1.0):
    I32 = mybir.dt.int32
    ch.step(eng.tensor_scalar(v, v, scale, EPS, ALU.mult, ALU.add))
    ch.step(eng.tensor_scalar(y.bitcast(I32), v.bitcast(I32), 1, None, ALU.arith_shift_right))
    ch.done(eng.tensor_scalar(v, v, -0.5, None, ALU.mult))
    ch.sync()
    ch.step(eng.tensor_scalar(y.bitcast(I32), y.bitcast(I32), -1.0, float(0x5F3759DF), ALU.mult, ALU.add))
    for _ in range(4):
        ch.step(eng.tensor_tensor(t, y, y, ALU.mult))
        ch.step(eng.tensor_tensor(t, t, v, ALU.mult))
        ch.step(eng.scalar_tensor_tensor(y, t, 1.5, y, ALU.add, ALU.mult))


def normalize(dve, st, mv, xn, tiles, ch, free):
    for i, t in enumerate(tiles):
        ch.done(dve.bn_stats(st[:, i, :], t))
    yield
    ch.sync()
    mean, var, d, rstd = (mv[:, i, :] for i in range(4))
    ch.done(dve.tensor_tensor(mean, st[:, :, 1], st[:, :, 4], ALU.add))
    ch.done(dve.tensor_tensor(var, st[:, :, 2], st[:, :, 5], ALU.add))
    ch.step(dve.tensor_tensor(d, st[:, :, 1], st[:, :, 4], ALU.subtract))
    ch.done(dve.tensor_scalar(mean, mean, 0.5, None, ALU.mult))
    ch.step(dve.scalar_tensor_tensor(d, d, 0.25, d, ALU.mult, ALU.mult))
    ch.step(dve.scalar_tensor_tensor(var, var, 1.0 / HID, d, ALU.mult, ALU.add))
    rsqrt(dve, ch, rstd, var, d)
    yield
    for i, t in enumerate(tiles):
        sem = free(i)
        dve.tensor_scalar(xn[:, i, :], t, mean[:, i:i + 1], rstd[:, i:i + 1], ALU.subtract, ALU.mult).then_inc(sem, 1)


def ffn(nc, s, tag, ug_s, dn_s, wsc, feed=None, out=None):
    res, cs, banks = s["res"], s["cs"], s["banks"]
    with ExitStack() as ctx:
        def sb(name, shape, dt=F32):
            return ctx.enter_context(nc.sbuf_tensor(f"f{tag}_{name}", shape, dt))

        def sem(name):
            return ctx.enter_context(nc.semaphore(f"f{tag}_{name}"))

        xT = sb("xT", [P, 2, KH, TOK], F32R)
        xn = s["xn"]
        st, mv = sb("st", [P, TPG, 6]), sb("mv", [P, 4, TPG])
        wu = [sb(f"wu{i}", [P, 2, KH, 2 * CH], F32R) for i in range(2)]
        wd = [sb(f"wd{i}", [P, 2, 2, HID], F32R) for i in range(2)]
        sc = [sb(f"sc{i}", [P, 4], F32) for i in range(2)]
        sil = sb("sil", [P, 2, 512])
        hf = sb("hf", [P, 2, 512])
        hb = sb("hb", [P, 2, 2, 2, 512], F32R)
        s_wu = [sem("wu0s"), sem("wu1s")]
        s_wd = [sem("wd0s"), sem("wd1s")]
        s_u, s_sil, s_h, s_hi, s_lo, s_d, s_acc = (sem(n) for n in ("u", "sils", "h", "hi", "lo", "d", "acc"))
        s_own, s_xn, s_tr, s_xhi, s_xlo = (sem(n) for n in ("own", "xns", "tr", "xhi", "xlo"))
        s_sc, s_out = [sem("sc0s"), sem("sc1s")], sem("out")
        if feed:
            wug, win, wout, in_s, out_s, x = feed
            s_x = sem("x")
            raw, t1 = xn, sb("t1", [P, KH, 2 * CH])
            mraw = sb("mraw", [P, 2, HID])
            msp = sb("msp", [P, 2, 2, HID], F32R)
            s_fr, s_fb, s_fm, s_fhi, s_flo, s_fs = (sem(n) for n in ("fr", "fb", "fm", "fhi", "flo", "fs"))
            s_mr, s_ms = [sem("mr0"), sem("mr1")], [sem("ms0"), sem("ms1")]
            s_mhi, s_mlo = sem("mhi"), sem("mlo")
        U, D, T = banks[0:4], banks[4:6], banks[6:8]

        def mixer_blocks(c):
            n = 4 * (c - 1)
            if isinstance(c, int) and n >= NIN + 1:
                return feed[2], feed[4], n - (NIN + 1)
            return feed[1], feed[3], n

        def transformed(c2, m):
            if not feed or (isinstance(c2, int) and (c2 == 0 and m < 4 or c2 == NC // 2 - 1 and m >= 4)):
                return ()
            return {1: (0, 1), 2: (2, 3)}.get(m % 4, ())

        block = ctx.enter_context(nc.Block())

        def over_chunks(eng, body):
            body(0)
            with eng.Fori(1, NC // 2 - (1 if feed else 0)) as c2:
                body(c2)
            if feed:
                body(NC // 2 - 1)

        @block.sync
        def _(sp):
            def dram(t, i):
                return t[bass.ds(i, 1)].rearrange("c p n -> (c p) n")

            def load(c, p, gate_up=True):
                wait(sp, s_d, 16 * (c - 1))
                wait(sp, s_sc[p], 0 if isinstance(c, int) else 16)
                if gate_up:
                    sp.dma_start(wu[p][:].rearrange("p h k n -> p (h k n)").bitcast(F32), dram(ug_s, c)).then_inc(s_wu[p], 16)
                sp.dma_start(sc[p][:], dram(wsc, c)).then_inc(s_sc[p], 16)
                sp.dma_start(wd[p][:].rearrange("p h k n -> p (h k n)").bitcast(F32), dram(dn_s, c)).then_inc(s_wd[p], 16)

            def beside(c, p):
                last = isinstance(c, int) and c == NC - 1
                if not last:
                    if isinstance(c, int) and c == 1:
                        sp.wait_ge(s_tr, NT)
                    else:
                        sp.wait_ge(s_fm, KH * (c - 1))
                        sp.wait_ge(s_sc[0], 16)
                    sp.dma_start(raw[:].rearrange("p k n -> p (k n)"), dram(wug, c + 1)).then_inc(s_fr, 16)
                    load(c + 1, 1 - p, gate_up=False)
                src, dst, at = mixer_blocks(c)

                def store_block(i):
                    sp.wait_ge(s_mlo, 4 * (c - 1) + i + 1)
                    sp.wait_ge(s_sc[0], 16)
                    sp.dma_start(dram(dst, at + i), msp[:, i % 2].rearrange("p h n -> p (h n)").bitcast(F32)).then_inc(s_ms[i % 2], 16)

                for i in range(4):
                    wait(sp, s_mlo, 4 * (c - 1) + i - 1)
                    sp.wait_ge(s_sc[0], 16)
                    sp.dma_start(mraw[:, i % 2], dram(src, at + i)).then_inc(s_mr[i % 2], 16)
                    if i:
                        store_block(i - 1)
                store_block(3)
                if not last:
                    sp.wait_ge(s_flo, KH * c)
                    sp.wait_ge(s_sc[0], 16)
                    sp.dma_start(dram(ug_s, c + 1), wu[1 - p][:].rearrange("p h k n -> p (h k n)").bitcast(F32)).then_inc(s_fs, 16)

            load(0, 0)
            if feed:
                sp.dma_start(res[:, 2 * TPG:NT, :], x.rearrange("(t p) n -> p t n", p=P)[:, 2 * TPG:NT, :]).then_inc(s_x, 16)
            load(1, 1)
            if feed:
                beside(1, 1)
                with sp.Fori(1, NC // 2 - 1) as c2:
                    beside(2 * c2, 0)
                    beside(2 * c2 + 1, 1)
                beside(NC - 2, 0)
                beside(NC - 1, 1)
                sp.wait_ge(s_fs, 16 * (NC - 2))
                for i in range(2):
                    sp.wait_ge(s_ms[i], 32 * (NC - 1))
            else:
                with sp.Fori(1, NC // 2) as c2:
                    load(2 * c2, 0)
                    load(2 * c2 + 1, 1)
            if out is not None:
                for g in range(G):
                    at = slice(g * 512, (g + 1) * 512)
                    sp.wait_ge(s_acc, TPG * (G * (NC - 1) + g + 1))
                    sp.dma_start(out[at].rearrange("(t p) n -> p t n", p=P), res[:, TPG * g:TPG * (g + 1), :]).then_inc(s_out, 16)
                sp.wait_ge(s_out, 16 * G)

        @block.tensor
        def _(pe):
            def turn(g, tiles=range(TPG)):
                for i in tiles:
                    t = TPG * g + i
                    if g:
                        pe.wait_ge(s_xn, t - TPG + 1)
                    wait(pe, s_xlo, t - 1)
                    for k in range(KH):
                        ins = pe.transpose(T[i % 2][:, k * P:(k + 1) * P], xn[:, i, k * P:(k + 1) * P], cs[:, C_I4:C_I4 + P])
                    ins.then_inc(s_tr, 1)

            def up(n, c2, m):
                g, p = m % 4, m // 4
                if isinstance(n, int) and n < 4:
                    pe.wait_ge(s_xlo, TPG * (g + 1))
                if g == 0:
                    if feed and not (isinstance(c2, int) and c2 == 0):
                        pe.wait_ge(s_flo, KH * (2 * c2 + p - 1))
                    else:
                        pe.wait_ge(s_wu[p], 16 * c2 + 16)
                for j in range(4):
                    wait(pe, s_sil if j < 2 else s_h, 2 * n - 1 + j % 2)
                    for k in range(KH):
                        for a, b in PASSES:
                            ins = pe.matmul(U[j][:], wu[p][:, a, k, j * P:(j + 1) * P], xT[:, b, k, g * 512:(g + 1) * 512],
                                            start=(k == 0 and (a, b) == PASSES[0]), stop=(k == KH - 1 and (a, b) == PASSES[-1]))
                    ins.then_inc(s_u, 1)
                    if isinstance(n, int) and n < 3 and j >= 2:
                        turn(n + 1, range(2 * (j - 2), 2 * (j - 1)))

            def down(n, c2, m):
                g, p = m % 4, m // 4
                if g == 0:
                    pe.wait_ge(s_wd[p], 16 * c2 + 16)
                pe.wait_ge(s_lo, 2 * n + 2)
                for t in range(TPG):
                    wait(pe, s_acc, 4 * n + t - 1)
                    for j in range(2):
                        for a, b in PASSES:
                            ins = pe.matmul(D[t % 2][:], hb[:, m % 2, a, j, t * P:(t + 1) * P], wd[p][:, b, j, :],
                                            start=(j == 0 and (a, b) == PASSES[0]), stop=(j == 1 and (a, b) == PASSES[-1]))
                    ins.then_inc(s_d, 1)

            def body(c2):
                first = isinstance(c2, int) and c2 == 0
                for m in range(8):
                    n = 8 * c2 + m
                    up(n, c2, m)
                    if m:
                        down(n - 1, c2, m - 1)
                    elif not first:
                        down(n - 1, c2 - 1, 7)
                    for k in transformed(c2, m):
                        at = KH * (2 * c2 + m // 4 - 1) + k
                        pe.wait_ge(s_fb, at - k + 4)
                        if isinstance(at, int) and at < 2:
                            pe.wait_ge(s_xlo, NT)
                        else:
                            pe.wait_ge(s_flo, at - 1)
                        pe.matmul(T[k % 2][:], cs[:, C_H:C_H + P], raw[:, k, :], start=True, stop=True).then_inc(s_fm, 1)
            turn(0)
            over_chunks(pe, body)
            down(4 * NC - 1, NC // 2 - 1, 7)

        @block.scalar
        def _(act):
            def turn(g, tiles=range(TPG)):
                for i in tiles:
                    t = TPG * g + i
                    act.wait_ge(s_tr, t + 1)
                    act.copy(xT[:, 0, :, t * P:(t + 1) * P], T[i % 2][:].rearrange("p (k n) -> p k n", k=KH)).then_inc(s_xhi, 1)

            def beside(c2, m):
                c = 2 * c2 + m // 4
                for k in transformed(c2, m):
                    at = KH * (c - 1) + k
                    act.wait_ge(s_fm, at + 1)
                    if k == 0:
                        wait(act, s_fs, 16 * (c - 1))
                    act.activation(wu[1 - m // 4][:, 0, k, :], T[k % 2][:], ACT.Copy, scale=s["sug"][:, k:k + 1]).then_inc(s_fhi, 1)
                i = m % 4
                turns = 2 * (c - 1) + i // 2
                act.wait_ge(s_mr[i % 2], 16 * turns + 16)
                wait(act, s_ms[i % 2], 16 * turns)
                _, dst, first = mixer_blocks(c)
                nw = P_NW + first + i if dst is out_s else None
                act.activation(msp[:, i % 2, 0, :], mraw[:, i % 2, :], ACT.Copy,
                               scale=1.0 if nw is None else s["pr"][:, nw:nw + 1]).then_inc(s_mhi, 1)

            def body(c2):
                first = isinstance(c2, int) and c2 == 0
                for m in range(8):
                    n, p = 8 * c2 + m, m // 4
                    if m % 4 == 0:
                        act.wait_ge(s_sc[p], 16 * c2 + 16)
                    for j in range(2):
                        act.wait_ge(s_u, 4 * n + j + 1)
                        wait(act, s_h, 2 * n - 1 + j)
                        act.activation(sil[:, j, :], U[j][:], ACT.Silu, scale=sc[p][:, j:j + 1]).then_inc(s_sil, 1)
                    if first and m < 3:
                        turn(m + 1, range(2))
                    for j in range(2):
                        act.wait_ge(s_h, 2 * n + j + 1)
                        wait(act, s_d, 4 * n - 4)
                        act.copy(hb[:, m % 2, 0, j, :], hf[:, j, :]).then_inc(s_hi, 1)
                    if first and m < 3:
                        turn(m + 1, range(2, TPG))
                    if feed and not (first and m < 4):
                        beside(c2, m)
            turn(0)
            over_chunks(act, body)

        @block.vector
        def _(dve):
            own = Chain(dve, s_own)

            def rows(g):
                def free(i):
                    wait(dve, s_tr, TPG * (g - 1) + i + 1)
                    return s_xn
                wait(dve, s_xn, TPG * (g - 1))
                if feed and g == 2:
                    dve.wait_ge(s_x, 16)
                run(normalize(dve, st, mv, xn, [res[:, TPG * g + i, :] for i in range(TPG)], own, free))

            def turn(g, tiles=range(TPG)):
                for i in tiles:
                    t = TPG * g + i
                    dve.wait_ge(s_xhi, t + 1)
                    at = slice(t * P, (t + 1) * P)
                    dve.tensor_tensor(xT[:, 1, :, at], T[i % 2][:].rearrange("p (k n) -> p k n", k=KH),
                                      xT[:, 0, :, at].bitcast(F32), ALU.subtract).then_inc(s_xlo, 1)

            def add(n, m):
                for t in range(TPG):
                    dve.wait_ge(s_d, 4 * n + t + 1)
                    r = res[:, TPG * (m % 4) + t, :]
                    dve.tensor_tensor(r, D[t % 2][:], r, ALU.add).then_inc(s_acc, 1)

            def beside(c2, m):
                c = 2 * c2 + m // 4
                for k in transformed(c2, m):
                    dve.wait_ge(s_fhi, KH * (c - 1) + k + 1)
                    to = wu[1 - m // 4]
                    dve.scalar_tensor_tensor(to[:, 1, k, :], T[k % 2][:], s["sug"][:, k:k + 1], to[:, 0, k, :].bitcast(F32),
                                             ALU.mult, ALU.subtract).then_inc(s_flo, 1)
                _, dst, first = mixer_blocks(c)
                if dst is out_s:
                    i = m % 4
                    nw = P_NW + first + i
                    dve.wait_ge(s_mhi, 4 * (c - 1) + i + 1)
                    dve.scalar_tensor_tensor(msp[:, i % 2, 1, :], mraw[:, i % 2, :], s["pr"][:, nw:nw + 1],
                                             msp[:, i % 2, 0, :].bitcast(F32), ALU.mult, ALU.subtract).then_inc(s_mlo, 1)

            def body(c2):
                first = isinstance(c2, int) and c2 == 0
                for m in range(8):
                    n, p = 8 * c2 + m, m // 4
                    if first and m < 3:
                        rows(m + 1)
                    if m % 4 == 0:
                        dve.wait_ge(s_sc[p], 16 * c2 + 16)
                    for j in range(2):
                        dve.wait_ge(s_sil, 2 * n + j + 1)
                        dve.wait_ge(s_u, 4 * n + j + 3)
                        wait(dve, s_hi, 2 * n - 1 + j)
                        wait(dve, s_lo, 2 * n - 1 + j)
                        dve.scalar_tensor_tensor(hf[:, j, :], U[2 + j][:], sc[p][:, 2 + j:3 + j], sil[:, j, :],
                                                 ALU.mult, ALU.mult).then_inc(s_h, 1)
                        if first and m < 3:
                            turn(m + 1, range(2 * j, 2 * j + 2))
                    if not (first and m == 0):
                        add(n - 1, (m - 1) % 8)
                    for j in range(2):
                        dve.wait_ge(s_hi, 2 * n + j + 1)
                        dve.tensor_tensor(hb[:, m % 2, 1, j, :], hf[:, j, :], hb[:, m % 2, 0, j, :].bitcast(F32),
                                          ALU.subtract).then_inc(s_lo, 1)
                    if feed and not (first and m < 4):
                        beside(c2, m)
                    if feed and isinstance(c2, int) and c2 == NC // 2 - 1 and m == 6:
                        dve.wait_ge(s_fm, KH * (NC - 2))
                        dve.wait_ge(s_acc, TPG * (G * (NC - 1) + 1))
                        run(normalize(dve, st, mv, xn, [res[:, i, :] for i in range(TPG)], own, lambda i: s_xn))
            turn(0)
            over_chunks(dve, body)
            add(4 * NC - 1, 7)

        if feed:
            @block.gpsimd
            def _(pool):
                def body(c2):
                    for p in range(2):
                        c = 2 * c2 + p
                        if isinstance(c, int) and c == 0:
                            continue
                        if not (isinstance(c, int) and c == NC - 1):
                            pool.wait_ge(s_fr, 16 * c)
                            for n, op in enumerate((ALU.add, ALU.subtract)):
                                pool.tensor_tensor(t1[:, n::2, :], raw[:, 0::2, :], raw[:, 1::2, :], op).then_inc(s_fb, 1)
                            pool.wait_ge(s_fb, 4 * (c - 1) + 2)
                            for n, op in enumerate((ALU.add, ALU.subtract)):
                                pool.tensor_tensor(raw[:, 2 * n:2 * n + 2, :], t1[:, 0:2, :], t1[:, 2:4, :], op).then_inc(s_fb, 1)
                        if mixer_blocks(c)[1] is in_s:
                            for i in range(4):
                                pool.wait_ge(s_mhi, 4 * (c - 1) + i + 1)
                                pool.tensor_tensor(msp[:, i % 2, 1, :], mraw[:, i % 2, :], msp[:, i % 2, 0, :].bitcast(F32),
                                                   ALU.subtract).then_inc(s_mlo, 1)
                over_chunks(pool, body)


def mixer(nc, s, in_s, out_s):
    res, cs, pr, banks, i2r, ones = s["res"], s["cs"], s["pr"], s["banks"], s["i2r"], s["ones"]
    RING = 4
    LCONV = 2 + NB
    POOL_M = {0: (1, 2, 3), 1: (1, 2, 3)}
    MIX = (5, 9, 12, 14, 15, 17, 19, 21, 25)
    FIRST = 5
    USES = ([("in", 0, n) for n in range(FIRST, NIN)] + [("in", 1, n) for n in range(FIRST)]
            + [("out", 0, b) for b in range(NB)])
    LEAD = [u for u in USES if u[1]]
    LAST = [u for u in USES if not u[1]]
    with ExitStack() as ctx:
        def sb(name, shape, dt=F32):
            return ctx.enter_context(nc.sbuf_tensor(f"m_{name}", shape, dt))

        def sem(name):
            return ctx.enter_context(nc.semaphore(f"ms_{name}"))

        xn, st, mv = s["xn"], sb("st", [P, TPG, 6]), sb("mv", [P, 4, TPG])
        xT = sb("xT", [P, 2, KH, SEQ], F32R)
        ring = [sb(f"w{i}", [P, 2, HID], F32R) for i in range(RING)]
        xr = sb("xr", [P, 2, SEQ + 4])
        cv = sb("cv", [P, 2, SEQ])
        xc, zs = sb("xc", [P, 2, SEQ]), sb("zs", [P, 2, SEQ])
        Bf, Cf = sb("Bf", [P, SEQ]), sb("Cf", [P, SEQ])
        du, de, dw, dl, dtf = (sb(n, [P, SEQ]) for n in ("du", "de", "dw", "dl", "dtf"))
        da = sb("da", [P, SEQ])
        ec = sb("ec", [P, SEQ])
        aS, eS = sb("aS", [P, SEQ], F32R), sb("eS", [P, SEQ], F32R)
        dg = sb("dg", [HEADS, 2, HEADS])
        GT = sb("GT", [P, SEQ])
        Bt = sb("Bt", [P, 3, STATE])
        dd = sb("dd", [P, 6 * HEADS])
        xp = sb("xp", [P, 2, NCK, HPB, 32])
        L = sb("L", [P, 2, 4, SEQ])
        xd = sb("xd", [P, 2, 3, P])
        sta = sb("sta", [P, 2, 3, P])
        ex, z, y = sb("ex", [P, 2, SEQ]), sb("z", [P, 2, SEQ]), sb("y", [P, 2, SEQ])
        yh = sb("yh", [P, NB, 2, SEQ], F32R)
        sq, ss = sb("sq", [P, SEQ]), sb("ss", [P, SEQ])
        rr = sb("rr", [P, 3 * TPG])
        i2x = sb("i2x", [P, INTER], F32R)
        (s_xn, s_tr, s_xhi, s_xlo, s_in, s_os, s_pev, s_cv, s_xcv, s_e, s_ln, s_a, s_ah, s_eh,
         s_nu, s_dw, s_dt, s_as, s_ec, s_es, s_dg, s_G, s_B, s_D, s_gt, s_bt, s_dd, s_X, s_xp, s_A, s_sc,
         s_xd, s_mv, s_mp, s_Y, s_S, s_st, s_O, s_E, s_ex, s_y, s_z, s_yf, s_ss, s_yh, s_yl, s_V, s_v,
         s_op, s_fin, s_own, s_po, s_z0, s_sq) = (sem(n) for n in (
             "xn tr xhi xlo in os pev cv xcv e ln a ah eh nu dw dt as ec es dg G B D gt bt dd X xp A sc "
             "xd mv mp Y S st O E ex y z yf ss yh yl V v op fin own po z0 sq").split())
        s_w = [sem(f"w{i}") for i in range(RING)]
        PB, A, Y, X, S, O = banks[0:2], banks[2:4], banks[4], banks[5], banks[6], banks[7]
        OUT = [PB[0], PB[1], S, Y]
        I = cs[:, C_I4:C_I4 + P]
        order = [BI_DT, BI_B, BI_C] + [i for b in range(NB) for i in (NB + b, b)]

        def ck(c):
            return slice(c * P, (c + 1) * P)

        def slot(use):
            return USES.index(use) % RING

        def loaded(q, use, uses):
            count = lambda some: sum(slot(u) == slot(use) for u in some)
            return 16 * (count(LEAD) + count(USES) * q + count(uses[:uses.index(use)]) + 1)

        def used(q, use):
            what, on, n = use
            if what == "in":
                return s_in, NIN * (q + on) + n + 1
            if n < NB - 1:
                return s_os, (NB - 1) * q + n + 1
            return s_op, TPG * (q + 1)

        block = ctx.enter_context(nc.Block())

        def over_sequences(eng, ahead, body):
            ahead(0)
            body(0, USES)
            with eng.Fori(1, BATCH - 1) as q:
                body(q, USES)
            body(BATCH - 1, LAST)

        @block.sync
        def _(sp):
            def load(use):
                what, _, n = use
                src = in_s[order[n]] if what == "in" else out_s[n]
                sp.dma_start(ring[slot(use)][:].rearrange("p h n -> p (h n)").bitcast(F32), src).then_inc(s_w[slot(use)], 16)

            def ahead(q):
                for i, use in enumerate(LEAD):
                    if i >= RING:
                        wait(sp, *used(-1, LEAD[i - RING]))
                    load(use)

            def body(q, uses):
                first = isinstance(q, int) and q == 0
                for use in uses:
                    before = [(q, u) for u in uses[:uses.index(use)] if slot(u) == slot(use)]
                    before = before or [(q - 1, u) for u in USES if slot(u) == slot(use) and (u in LEAD or not first)]
                    if before:
                        wait(sp, *used(*before[-1]))
                    load(use)
            over_sequences(sp, ahead, body)

        @block.tensor
        def _(pe):
            def in_proj(q, n, value):
                at = slot(("in", int(n < FIRST), n))
                w = ring[at][:].rearrange("p h (k m) -> p h k m", k=KH)
                for k in range(KH):
                    for i, (a, b) in enumerate(PASSES):
                        if k == 0 and i == 0:
                            pe.wait_ge(s_w[at], value)
                            pe.wait_ge(s_xlo, TPG * (q + 1))
                            wait(pe, s_pev, NIN * q + n - 1 if n >= 2 else NIN * q)
                        ins = pe.matmul(PB[n % 2][:], w[:, a, k, :], xT[:, b, k, :],
                                        start=(k == 0 and i == 0), stop=(k == KH - 1 and i == 2))
                        if k == KH - 1 and i == 2:
                            ins.then_inc(s_in, 1)
                        yield

            def turn(q):
                for i in range(TPG):
                    if not (isinstance(q, int) and q == 0):
                        pe.wait_ge(s_xn, TPG * (q - 1) + i + 1)
                    wait(pe, s_xlo, TPG * q + i - 1)
                    wait(pe, s_pev, NIN * q)
                    for k in range(KH):
                        ins = pe.transpose(PB[i % 2][:, ck(k)], xn[:, i, ck(k)], I)
                    ins.then_inc(s_tr, 1)

            def prepare_heads(q):
                pe.wait_ge(s_xcv, LCONV * q + 2)
                wait(pe, s_z, NB * q)
                for c in range(NCK):
                    ins = pe.matmul(O[:, ck(c)], Bf[:, ck(c)], Cf[:, ck(c)], start=True, stop=True)
                ins.then_inc(s_G, 1)
                yield
                pe.wait_ge(s_gt, q + 1)
                for c in range(3):
                    ins = pe.transpose(O[:, ck(c)], Bf[:, ck(c)], I)
                ins.then_inc(s_B, 1)
                yield
                pe.wait_ge(s_dt, q + 1)
                wait(pe, s_ex, NB * q)
                pe.wait_ge(s_dg, q + 1)
                for i in range(2):
                    pe.matmul(X[:, HEADS * (4 + i):HEADS * (5 + i)], ones[0:HEADS, :], dg[:, i, :], start=True, stop=True)
                for c in range(NCK):
                    ins = pe.transpose(X[:, HEADS * c:HEADS * (c + 1)], dtf[0:HEADS, ck(c)], cs[0:HEADS, C_I4:C_I4 + HEADS])
                ins.then_inc(s_D, 1)

            def decays(q, n):
                if n == 0:
                    pe.wait_ge(s_as, q + 1)
                wait(pe, s_sc, 64 * q + n - 1)
                h = n // 8 * HPB + 2 * (n % 4) + n // 4 % 2
                pe.matmul(A[n % 2][:], i2r[:, h:h + 1].to_broadcast([P, P]), aS[:], start=True, stop=True).then_inc(s_A, 1)

            def x_rows(q, b):
                pe.wait_ge(s_xcv, LCONV * q + 2 + b + 1)
                if b == 0:
                    pe.wait_ge(s_dd, q + 1)
                elif b == 1:
                    pe.wait_ge(s_xp, NB * q + 1)
                else:
                    pe.wait_ge(s_ex, NB * q + b - 1)
                for c in range(NCK):
                    ins = pe.transpose(X[:, ck(c)], xc[:, b % 2, ck(c)], I)
                ins.then_inc(s_X, 1)

            def head(q):
                yield from prepare_heads(q)
                yield
                x_rows(q, 0)
                for n in range(6):
                    decays(q, n)
                    yield

            def ahead(q):
                turn(q)
                for use in LEAD:
                    run(in_proj(q, use[2], loaded(q - 1, use, USES) if not isinstance(q, int) or q else
                                16 * (sum(slot(u) == slot(use) for u in LEAD[:LEAD.index(use)]) + 1)))
                run(head(q))

            def body(q, uses):
                def ydiag(qd):
                    b, e = qd // 2, qd % 2
                    if e == 0:
                        wait(pe, s_y, NB * q + b)
                    pe.wait_ge(s_xp, NB * q + b + 1)
                    pe.wait_ge(s_mv, 2 * NB * q + qd + 1)
                    pe.wait_ge(s_mp, 2 * NB * q + qd + 1)
                    for c in range(NCK):
                        for j in range(4):
                            ins = pe.matmul(Y[32 * j:32 * j + 32, ck(c)], xp[:, b % 2, c, 2 * j + e, :], L[:, e, j, ck(c)],
                                            start=(e == 0 and c == 0), stop=(e == 1), skip_group_check=True)
                    ins.then_inc(s_Y, 1)

                def new_states(b):
                    pe.wait_ge(s_xd, 2 * (NB * q + b + 1))
                    if b:
                        pe.wait_ge(s_st, NB * q + b)
                    else:
                        pe.wait_ge(s_bt, q + 1)
                    for c in range(3):
                        ins = pe.matmul(S[:, ck(c)], Bt[:, c, :], xd[:, b % 2, c, :], start=True, stop=True)
                    ins.then_inc(s_S, 1)

                def tail(b):
                    ydiag(2 * b + 1)
                    if b < NB - 1:
                        pe.wait_ge(s_xp, NB * q + b + 2)
                    else:
                        pe.wait_ge(s_ex, NB * q + b)
                    if b == 0:
                        pe.wait_ge(s_es, q + 1)
                    pe.matmul(X[:], i2x[:, ck(b)], eS[:], start=True, stop=True).then_inc(s_E, 1)
                    pe.wait_ge(s_st, NB * q + b + 1)
                    wait(pe, s_z, NB * q + b)
                    if b == 0:
                        wait(pe, s_v, q)
                    for c in range(1, NCK):
                        ins = pe.matmul(O[:, ck(c)], sta[:, b % 2, c - 1, :], Cf[:, ck(c)], start=True, stop=True)
                    ins.then_inc(s_O, 1)

                def fills(i):
                    ins = [u for u in uses if u[0] == "in"]
                    if i >= len(ins):
                        return iter(())
                    return in_proj(q + ins[i][1], ins[i][2], loaded(q, ins[i], uses))

                more = uses is USES
                for b in range(NB):
                    if b:
                        x_rows(q, b)
                    else:
                        wait(pe, s_fin, TPG * q)
                    if b == NB - 1 and more:
                        turn(q + 1)
                    for e in range(2):
                        fill = fills(2 * b + e)
                        n = 8 * b + 4 * e
                        if e == 0 and b:
                            new_states(b - 1)
                        for j in range(2, 6):
                            if n == 0:
                                due = 2 + j if j >= 4 else None
                            else:
                                due = n + j if 8 <= n + j < 8 * NB else None
                            if due:
                                decays(q, due)
                            for _ in range(2):
                                next(fill, None)
                        run(fill)
                        if e == 1:
                            ydiag(2 * b)
                        elif b:
                            tail(b - 1)
                run(fills(2 * NB))
                new_states(NB - 1)
                tail(NB - 1)
                run(fills(2 * NB + 1))
                run(fills(2 * NB + 2))
                pe.wait_ge(s_pev, NIN * q + NIN + (FIRST if more else 0))
                pe.wait_ge(s_st, NB * (q + 1))
                pe.wait_ge(s_y, NB * (q + 1))
                following = head(q + 1) if more else iter(())
                for b in range(NB):
                    at = slot(("out", 0, b))
                    pe.wait_ge(s_w[at], loaded(q, ("out", 0, b), uses))
                    pe.wait_ge(s_yl, NB * q + b + 1)
                    if b == NB - 2:
                        pe.wait_ge(s_ss, (NB - 1) * (q + 1))
                        pe.wait_ge(s_z, NB * (q + 1))
                        if more:
                            pe.wait_ge(s_bt, q + 2)
                        for t in range(TPG):
                            ins = pe.matmul(O[:, t:t + 1], ss[:, ck(t)], ones[:, 0:1], start=True, stop=True)
                        ins.then_inc(s_V, 1)
                    for t in range(TPG):
                        for i, (m, n) in enumerate(PASSES):
                            ins = pe.matmul(OUT[t][:], yh[:, b, m, ck(t)], ring[at][:, n, :],
                                            start=(b == 0 and i == 0), stop=(b == NB - 1 and i == 2))
                        if b == NB - 1:
                            ins.then_inc(s_op, 1)
                        elif t == TPG - 1:
                            ins.then_inc(s_os, 1)
                        if TPG * b + t in MIX:
                            next(following, None)
                run(following)
            over_sequences(pe, ahead, body)

        @block.scalar
        def _(act):
            def raw(q, n, col):
                at = (1, 2)[n] if n < 2 else 3 + 2 * (n - 2)
                act.wait_ge(s_in, NIN * q + at + 1)
                wait(act, s_cv, LCONV * q + n - 1)
                wait(act, s_xcv, LCONV * q + n - 1)
                act.copy(xr[:, n % 2, 3:3 + SEQ], PB[at % 2][:])
                w = P_CW + 4 * col
                act.activation(cv[:, n % 2, :], PB[at % 2][:], ACT.Identity, scale=pr[:, w + 3:w + 4],
                               bias=pr[:, P_CB + col:P_CB + col + 1]).then_inc(s_pev, 1)

            def conv_silu(q, n, dst):
                act.wait_ge(s_cv, LCONV * q + n + 1)
                act.activation(dst, cv[:, n % 2, :], ACT.Silu).then_inc(s_xcv, 1)

            def x_silu(q, b):
                wait(act, s_X, NB * q + b - 1)
                wait(act, s_y, NB * q + b - 1)
                conv_silu(q, 2 + b, xc[:, b % 2, :])

            def gate(q, b):
                act.wait_ge(s_in, NIN * q + 5 + 2 * b)
                wait(act, s_yf, NB * q + b - 1)
                act.activation(zs[:, b % 2, :], PB[(4 + 2 * b) % 2][:], ACT.Silu).then_inc(s_pev, 1)

            def turn(q):
                for i in range(TPG):
                    act.wait_ge(s_tr, TPG * q + i + 1)
                    wait(act, s_in, NIN * q)
                    act.copy(xT[:, 0, :, ck(i)], PB[i % 2][:].rearrange("p (k n) -> p k n", k=KH)).then_inc(s_xhi, 1)

            def times(q, b):
                act.wait_ge(s_E, NB * q + b + 1)
                wait(act, s_z, NB * q + b - 1)
                act.copy(ex[:, b % 2, :], X[:]).then_inc(s_ex, 1)

            def high(q, b):
                act.wait_ge(s_yf, NB * q + b + 1)
                wait(act, s_op, TPG * q)
                act.copy(yh[:, b, 0, :], y[:, b % 2, :]).then_inc(s_yh, 1)
                if b == 0:
                    wait(act, s_V, q)
                else:
                    wait(act, s_ss, (NB - 1) * q + b - 1)
                act.activation((sq if b else ss)[:], y[:, b % 2, :], ACT.Square).then_inc(s_sq, 1)

            def first(q, between):
                act.wait_ge(s_in, NIN * q + 1)
                wait(act, s_dt, q)
                act.activation(du[:], PB[0][:], ACT.Identity, bias=pr[:, P_DTB:P_DTB + 1]).then_inc(s_pev, 1)
                raw(q, 0, NB)
                act.wait_ge(s_nu, q + 1)
                act.activation(de[:], de[:], ACT.Exp).then_inc(s_e, 1)
                raw(q, 1, NB + 1)
                next(between, None)
                act.wait_ge(s_dw, q + 1)
                act.activation(dl[:], dw[:], ACT.Ln).then_inc(s_ln, 1)
                wait(act, s_O, NB * q)
                conv_silu(q, 0, Bf[:])
                raw(q, 2, 0)
                conv_silu(q, 1, Cf[:])
                gate(q, 0)
                act.wait_ge(s_dt, q + 1)
                wait(act, s_as, q)
                act.activation(da[:], dtf[:], ACT.Exp, scale=s["acol"][:, 0:1]).then_inc(s_a, 1)
                act.wait_ge(s_a, q + 1)
                wait(act, s_A, 64 * q)
                act.copy(aS[:], da[:]).then_inc(s_ah, 1)
                x_silu(q, 0)
                act.wait_ge(s_G, q + 1)
                wait(act, s_mp, 2 * NB * q)
                wait(act, s_mv, 2 * NB * q)
                act.copy(GT[:], O[:]).then_inc(s_gt, 1)
                act.wait_ge(s_ec, q + 1)
                wait(act, s_E, NB * q)
                act.copy(eS[:], ec[:]).then_inc(s_eh, 1)
                act.wait_ge(s_B, q + 1)
                act.copy(Bt[:].rearrange("p c n -> p (c n)"), O[:, 0:3 * P]).then_inc(s_bt, 1)

            def ahead(q):
                turn(q)
                first(q, iter(()))

            def body(q, uses):
                more = uses is USES

                def ending():
                    high(q, NB - 2)
                    times(q, NB - 1)
                    yield
                    high(q, NB - 1)
                    yield

                for b in range(NB):
                    if b < NB - 1:
                        raw(q, 3 + b, b + 1)
                    elif more:
                        turn(q + 1)
                    if b >= 2:
                        high(q, b - 2)
                    if b:
                        times(q, b - 1)
                    if b < NB - 1:
                        x_silu(q, b + 1)
                        gate(q, b + 1)
                end = ending()
                if more:
                    first(q + 1, end)
                run(end)
            over_sequences(act, ahead, body)

        @block.vector
        def _(dve):
            dve.memset(xp[:], 0.0).then_inc(s_z0, 1)
            dve.memset(xr[:, :, 0:3], 0.0).then_inc(s_z0, 1)
            dve.tensor_copy(i2x[:].rearrange("p (h d) -> p h d", d=HDIM),
                            cs[:, C_I2:C_I2 + HEADS].unsqueeze(2).to_broadcast([P, HEADS, HDIM])).then_inc(s_z0, 1)
            dve.wait_ge(s_z0, 3)
            counts = {}

            def tiles(q):
                return [res[:, bass.ds(TPG * q + i, 1), :].rearrange("p o n -> p (o n)") for i in range(TPG)]

            def rows(q, own):
                def free(i):
                    wait(dve, s_tr, TPG * (q - 1) + i + 1)
                    return s_xn
                if isinstance(q, int) and q == BATCH:
                    return normalize(dve, st, mv, xn, tiles(0), own, free)
                return normalize(dve, st, mv, xn, tiles(q), own, free)

            def turn(q):
                for i in range(TPG):
                    dve.wait_ge(s_xhi, TPG * q + i + 1)
                    dve.tensor_tensor(xT[:, 1, :, ck(i)], PB[i % 2][:].rearrange("p (k n) -> p k n", k=KH),
                                      xT[:, 0, :, ck(i)].bitcast(F32), ALU.subtract).then_inc(s_xlo, 1)

            def conv(q, n, col, own):
                dve.wait_ge(s_pev, NIN * q + ((1, 2)[n] if n < 2 else 3 + 2 * (n - 2)) + 1)
                w = P_CW + 4 * col
                for k in range(3):
                    ins = dve.scalar_tensor_tensor(cv[:, n % 2, :], xr[:, n % 2, k:k + SEQ], pr[:, w + k:w + k + 1],
                                                   cv[:, n % 2, :], ALU.mult, ALU.add)
                    if k < 2:
                        own.step(ins)
                ins.then_inc(s_cv, 1)

            def quad_scans(q, qd):
                for j in range(4):
                    n = 4 * qd + j
                    dve.wait_ge(s_A, 64 * q + n + 1)
                    wait(dve, s_Y, 2 * NB * q + qd - 1)
                    dve.tensor_tensor_scan(L[:, qd % 2, j, :], A[n % 2][:], cs[:, C_I4:C_I4 + SEQ], 0.0,
                                           ALU.mult, ALU.add).then_inc(s_sc, 1)

            def padded(q, b):
                dve.wait_ge(s_X, NB * q + b + 1)
                wait(dve, s_Y, 2 * (NB * q + b - 1))
                xv = X[:].rearrange("p (c j e d) -> p c j e d", c=NCK, j=4, e=2)
                dv = dd[:, 0:NCK * HEADS].rearrange("p (c h) -> p c h", c=NCK)
                pv = xp[:, b % 2].rearrange("p c (j e) m -> p c j e m", e=2)
                for e in range(2):
                    dt = dv[:, :, HPB * b + e:HPB * (b + 1):2].unsqueeze(3).to_broadcast([P, NCK, 4, HDIM])
                    ins = dve.tensor_tensor(pv[:, :, :, e, HDIM * e:HDIM * (e + 1)], xv[:, :, :, e, :], dt, ALU.mult)
                ins.then_inc(s_xp, 1)

            def decayed(q, qd):
                b, e = qd // 2, qd % 2
                dve.wait_ge(s_sc, 64 * q + 4 * qd + 4)
                dve.wait_ge(s_xp, NB * q + b + 1)
                wait(dve, s_S, NB * q + b - 1)
                pv = xp[:, b % 2].rearrange("p c (j e) m -> p c j e m", e=2)[:, 0:3, :, e, HDIM * e:HDIM * (e + 1)]
                last = L[:, e].rearrange("p j (c l) -> p c j l", c=NCK)[:, 0:3, :, P - 1:P].to_broadcast([P, 3, 4, HDIM])
                out = xd[:, b % 2].rearrange("p c (j e d) -> p c j e d", j=4, e=2)[:, :, :, e, :]
                dve.tensor_tensor(out, pv, last, ALU.mult).then_inc(s_xd, 1)

            def times_g(q, qd):
                e = qd % 2
                dve.wait_ge(s_xd, 2 * NB * q + qd + 1)
                for j in range(4):
                    if j not in POOL_M[e]:
                        ins = dve.tensor_tensor(L[:, e, j, :], L[:, e, j, :], GT[:], ALU.mult)
                ins.then_inc(s_mv, 1)

            def even_heads(q, b):
                quad_scans(q, 2 * b)
                padded(q, b)
                decayed(q, 2 * b)
                times_g(q, 2 * b)

            def first(q, own, between):
                dve.wait_ge(s_pev, NIN * q + 1)
                wait(dve, s_es, q)
                dve.scalar_tensor_tensor(de[:], du[:], -1.0, du[:], ALU.mult, ALU.min).then_inc(s_nu, 1)
                conv(q, 0, NB, own)
                next(between, None)
                dve.wait_ge(s_e, q + 1)
                dve.tensor_scalar(dw[:], de[:], 1.0, None, ALU.add).then_inc(s_dw, 1)
                conv(q, 1, NB + 1, own)
                dve.wait_ge(s_dw, q + 1)
                own.step(dve.scalar_tensor_tensor(de[:], dw[:], -1.0, de[:], ALU.add, ALU.subtract))
                wait(dve, s_D, q)
                own.step(dve.reciprocal(dtf[:], dw[:]))
                own.step(dve.tensor_tensor(de[:], de[:], dtf[:], ALU.mult))
                dve.wait_ge(s_ln, q + 1)
                own.step(dve.tensor_tensor(dl[:], dl[:], de[:], ALU.subtract))
                own.step(dve.scalar_tensor_tensor(dl[:], du[:], 0.0, dl[:], ALU.max, ALU.add))
                dve.tensor_scalar(dtf[:], dl[:], 100.0, 0.0, ALU.min, ALU.max).then_inc(s_dt, 1)
                next(between, None)
                dve.wait_ge(s_a, q + 1)
                wait(dve, s_eh, q)
                for c in range(NCK):
                    ins = dve.tensor_tensor_scan(ec[:, ck(c)], da[:, ck(c)], ones[:], 1.0, ALU.mult, ALU.mult)
                ins.then_inc(s_ec, 1)
                dve.wait_ge(s_ah, q + 1)
                own.step(dve.tensor_tensor(aS[HEADS:P, :], da[HEADS:P, :], aS[HEADS:P, :].bitcast(F32), ALU.subtract))
                dve.memset(aS[:, 0:SEQ:P].bitcast(F32), 0.0).then_inc(s_as, 1)
                dve.wait_ge(s_ec, q + 1)
                for i in range(2):
                    at = (i + 2) * P - 1
                    ins = dve.tensor_scalar(dg[:, i, :], cs[0:HEADS, C_I2:C_I2 + HEADS], ec[0:HEADS, at:at + 1], None, ALU.mult)
                ins.then_inc(s_dg, 1)
                conv(q, 2, 0, own)
                next(between, None)
                dve.wait_ge(s_eh, q + 1)
                dve.tensor_tensor(eS[HEADS:P, :], ec[HEADS:P, :], eS[HEADS:P, :].bitcast(F32), ALU.subtract).then_inc(s_es, 1)
                dve.wait_ge(s_D, q + 1)
                wait(dve, s_st, NB * q)
                dve.tensor_copy(dd[:], X[:, 0:6 * HEADS]).then_inc(s_dd, 1)
                dve.wait_ge(s_gt, q + 1)
                dve.wait_ge(s_dd, q + 1)
                even_heads(q, 0)
                run(between)
                quad_scans(q, 1)

            def ahead(q):
                own = Chain(dve, s_own)
                turn(q)
                first(q, own, iter(()))
                counts["ahead"] = own.n

            def body(q, uses):
                more = uses is USES
                own = Chain(dve, s_own, counts["ahead"] + counts.get("turn", 0) * q)

                def states(b):
                    dve.wait_ge(s_S, NB * q + b + 1)
                    wait(dve, s_O, NB * q + b - 1)
                    own.step(dve.tensor_copy(sta[:, b % 2, 0, :], S[:, ck(0)]))
                    for i in range(2):
                        at = HEADS * (4 + i) + HPB * b
                        decay = dd[:, at:at + HPB].unsqueeze(2).to_broadcast([P, HPB, HDIM])
                        own.step(dve.tensor_tensor(sta[:, b % 2, i + 1, :].rearrange("p (h d) -> p h d", h=HPB),
                                                   sta[:, b % 2, i, :].rearrange("p (h d) -> p h d", h=HPB), decay, ALU.mult))
                        ins = dve.tensor_tensor(sta[:, b % 2, i + 1, :], S[:, ck(i + 1)], sta[:, b % 2, i + 1, :], ALU.add)
                        if i == 0:
                            own.step(ins)
                    ins.then_inc(s_st, 1)

                def within(b):
                    dve.wait_ge(s_Y, 2 * (NB * q + b + 1))
                    wait(dve, s_sq, NB * q + b - 1)
                    wait(dve, s_yh, NB * q + b - 1)
                    wait(dve, s_yl, NB * q + b - 1)
                    dve.scalar_tensor_tensor(y[:, b % 2, :], xc[:, b % 2, :], pr[:, P_D + b:P_D + b + 1], Y[:],
                                             ALU.mult, ALU.add).then_inc(s_y, 1)

                def carried(b):
                    wait(dve, s_yf, NB * q + b - 1)
                    dve.wait_ge(s_O, NB * q + b + 1)
                    dve.wait_ge(s_ex, NB * q + b + 1)
                    dve.tensor_tensor(z[:, b % 2, P:SEQ], O[:, P:SEQ], ex[:, b % 2, P:SEQ], ALU.mult).then_inc(s_z, 1)

                def ending():
                    states(NB - 1)
                    yield
                    within(NB - 1)
                    carried(NB - 1)
                    yield
                    yield
                    dve.wait_ge(s_V, q + 1)
                    dve.tensor_copy(rr[:, 0:TPG], O[:, 0:TPG]).then_inc(s_v, 1)
                    dve.wait_ge(s_v, q + 1)
                    rsqrt(dve, own, rr[:, TPG:2 * TPG], rr[:, 0:TPG], rr[:, 2 * TPG:3 * TPG], 1.0 / INTER)
                    for t, tile in enumerate(tiles(q)):
                        dve.wait_ge(s_op, TPG * q + t + 1)
                        dve.scalar_tensor_tensor(tile, OUT[t][:], rr[:, TPG + t:TPG + t + 1], tile,
                                                 ALU.mult, ALU.add).then_inc(s_fin, 1)
                    yield

                following = rows(q + 1 if more else BATCH, own)
                for b in range(NB):
                    if b == NB - 1 and more:
                        turn(q + 1)
                    if b:
                        even_heads(q, b)
                    if b:
                        states(b - 1)
                        within(b - 1)
                    if b:
                        quad_scans(q, 2 * b + 1)
                    decayed(q, 2 * b + 1)
                    times_g(q, 2 * b + 1)
                    if b < NB - 1:
                        conv(q, 3 + b, b + 1, own)
                    if b:
                        carried(b - 1)
                    if b in (3, 4, 5):
                        next(following, None)
                end = ending()
                if more:
                    first(q + 1, own, end)
                run(end)
                counts.setdefault("turn", own.n)
            over_sequences(dve, ahead, body)

        @block.gpsimd
        def _(pool):
            def times_g(q, qd):
                e = qd % 2
                if qd == 0:
                    pool.wait_ge(s_gt, q + 1)
                pool.wait_ge(s_xd, 2 * NB * q + qd + 1)
                for j in POOL_M[e]:
                    ins = pool.tensor_tensor(L[:, e, j, :], L[:, e, j, :], GT[:], ALU.mult)
                ins.then_inc(s_mp, 1)

            def body(q, uses):
                own = Chain(pool, s_po, NB * q)

                def combine(b):
                    pool.wait_ge(s_z, NB * q + b + 1)
                    v = y[:, b % 2, :]
                    own.step(pool.tensor_tensor(y[:, b % 2, P:SEQ], y[:, b % 2, P:SEQ], z[:, b % 2, P:SEQ], ALU.add))
                    pool.wait_ge(s_pev, NIN * q + 5 + 2 * b)
                    pool.tensor_tensor(v, v, zs[:, b % 2, :], ALU.mult).then_inc(s_yf, 1)

                def add_squares(b):
                    pool.wait_ge(s_sq, NB * q + b + 1)
                    wait(pool, s_ss, (NB - 1) * q + b - 1)
                    pool.tensor_tensor(ss[:], ss[:], sq[:], ALU.add).then_inc(s_ss, 1)

                def low(b):
                    pool.wait_ge(s_yh, NB * q + b + 1)
                    pool.tensor_tensor(yh[:, b, 1, :], y[:, b % 2, :], yh[:, b, 0, :].bitcast(F32), ALU.subtract).then_inc(s_yl, 1)

                for b in range(NB):
                    if b:
                        times_g(q, 2 * b)
                    if b >= 2:
                        low(b - 2)
                    if b >= 3:
                        add_squares(b - 2)
                    times_g(q, 2 * b + 1)
                    if b:
                        combine(b - 1)
                low(NB - 2)
                add_squares(NB - 2)
                combine(NB - 1)
                low(NB - 1)
                add_squares(NB - 1)
                if uses is USES:
                    times_g(q + 1, 0)
            over_sequences(pool, lambda q: times_g(q, 0), body)


def kernel(**inputs):
    import concourse.bacc as _bacc
    from concourse.bass_utils import run_bass_kernel_spmd as _run

    I = {k.split("_", 1)[1]: np.asarray(v) for k, v in inputs.items()}
    f = np.float32

    def cols(v):
        return np.ascontiguousarray(v.reshape(-1, P).T)

    def rows(wT):
        K, N = wT.shape
        return wT.reshape(K // P, P, N).transpose(1, 0, 2).reshape(P, -1)

    gate, up = I["ffn_W_gate"], I["ffn_W_up"]
    wug = np.stack([rows(np.concatenate([w[c * CH:(c + 1) * CH] for w in (gate, up)]).T) for c in range(NC)])
    sc = I["ffn_Wscale_ug"]
    wsc = np.stack([np.concatenate([cols(sc[o + c * CH:o + (c + 1) * CH]) for o in (FF, 0)], 1) for c in range(NC)])
    wdn = rows(I["ffn_W_down"].T)
    w = I["attn_in_proj_w"]
    w = np.concatenate([w, w[-HEADS:], np.zeros((P, HID), f)])
    win = np.stack([rows(w[b * P:(b + 1) * P].T) for b in range(NIN + 1)])
    wout = I["attn_out_proj_w"].T.reshape(NB, P, HID)
    had = np.ones((1, 1), f)
    while had.shape[0] < P:
        had = np.block([[had, had], [had, -had]])
    eye = np.eye(P, dtype=f)
    cst = np.concatenate([had, np.tile(eye, (1, 4)), np.tile(np.eye(HEADS, dtype=f), (2, 1))], 1)
    par = np.concatenate([
        cols(I["ffn_SU_ug"]), cols(I["ffn_SU_dp"]),
        np.tile(I["attn_A_log"], 2)[:, None], np.tile(I["attn_dt_bias"], 2)[:, None],
        cols(np.repeat(I["attn_D"], HDIM)),
        I["attn_conv_w"].reshape(10, P, 4).transpose(1, 0, 2).reshape(P, 40), cols(I["attn_conv_b"]),
        cols(I["attn_norm_w"]), np.broadcast_to(I["ffn_Wscale_dp"], (P, HID))], 1)
    arrays = dict(x=I["attn_hidden_states"].reshape(TOK, HID), wug=wug, wsc=wsc, wdn=wdn, win=win, wout=wout, cst=cst, par=par)

    nc = _bacc.Bacc("TRN2", target_bir_lowering=False, num_devices=1)
    arrays = {f"in_{k}": np.ascontiguousarray(v) for k, v in arrays.items()}
    args = [nc.dram_tensor(k, v.shape, F32, kind="ExternalInput").ap() for k, v in arrays.items()]
    args.append(nc.dram_tensor("out", (TOK, HID), F32, kind="ExternalOutput").ap())
    program(nc, *args)
    r = _run(nc, [arrays], core_ids=[0])
    return r.results[0]["out"].reshape(BATCH, SEQ, HID)
```
